# Optimizing a Trainium2 kernel written in Bass

```python
import numpy as np
import jax
import jax.numpy as jnp

def _softmax(x, axis=-1):
    return jax.nn.softmax(x, axis=axis)

def _gelu(x):
    return jax.nn.gelu(x, approximate=True)

def _silu(x):
    return jax.nn.silu(x)

def _sigmoid(x):
    return jax.nn.sigmoid(x)

def _layernorm(x, axis=-1, eps=1e-05):
    m = jnp.mean(x, axis=axis, keepdims=True)
    v = jnp.var(x, axis=axis, keepdims=True)
    return (x - m) / jnp.sqrt(v + eps)

def _scatter_add(tgt, idx, src, axis=0):
    return tgt.at[idx].add(src)

def _segment_sum(src, seg, n):
    return jax.ops.segment_sum(src, seg, n)
kernel_name = 'mk_gnn_preln_d2_gnn_r32_7ff68d'

def setup_inputs(seed: int=0):
    np.random.seed(seed)
    _w = jnp.asarray

    def _rec_inputs():
        import jax
        import jax.numpy as jnp
        _gk = jax.random.key(seed)
        x = -0.0002928 + 1 * jax.random.normal(jax.random.fold_in(_gk, 1), (256, 512), jnp.float32)
        _s = jax.random.randint(jax.random.fold_in(_gk, 2), (2048,), 0, 256, jnp.int32)
        _d = jax.random.randint(jax.random.fold_in(_gk, 3), (2048,), 0, 256, jnp.int32)
        _loop = jnp.arange(256, dtype=jnp.int32)
        src = jnp.concatenate([_s, _d, _loop])
        dst = jnp.concatenate([_d, _s, _loop])
        _o = jnp.argsort(dst, stable=True)
        src = src[_o]
        dst = dst[_o]
        return (x, src, dst)
    x, src, dst = _rec_inputs()

    def _L0_gnn_setup():
        import jax, jax.numpy as jnp
        import numpy as np
        N = 256
        D = 512
        E = 8192
        STEPS = 3
        key = jax.random.key(seed)
        k1, k2, k3 = jax.random.split(key, 3)
        x = jax.random.normal(k1, (N, D), dtype=jnp.float32)
        edge_index = jax.random.randint(k2, (2, E), 0, N, dtype=jnp.int32)
        W = jax.random.normal(k3, (D, D), dtype=jnp.float32) / np.sqrt(D)
        b = jnp.zeros((D,), dtype=jnp.float32)
        diffusion_weights = jnp.ones((STEPS + 1,), dtype=jnp.float32) / (STEPS + 1)
        return {'x': x, 'edge_index': edge_index, 'W': W, 'b': b, 'diffusion_weights': diffusion_weights}
    _L0_gnn_all = _L0_gnn_setup()
    _L0_gnn_in = {k: v for k, v in _L0_gnn_all.items() if k in ('W', 'b', 'diffusion_weights')}
    del _L0_gnn_all

    def _L1_gnn_setup():
        import jax, jax.numpy as jnp
        import numpy as np
        N = 10000
        D = 512
        H = 4 * D
        E = 5000
        K = 8
        DELTA = D // K

        def _gcn_conv(x, W, b, src, dst, norm, n):
            msgs = x[src] * norm[:, None]
            agg = jax.ops.segment_sum(msgs, dst, num_segments=n)
            return agg @ W + b
        key = jax.random.key(seed)
        k0, k1, k2, k3, k4, k5 = jax.random.split(key, 6)
        x_all = jax.random.normal(k0, (N, D), dtype=jnp.float32)
        edge_index = jax.random.randint(k1, (2, E), 0, N, dtype=jnp.int64)
        s1 = 1.0 / np.sqrt(D)
        s2 = 1.0 / np.sqrt(H)
        W1 = jax.random.uniform(k2, (D, H), jnp.float32, -s1, s1)
        b1 = jnp.zeros((H,), jnp.float32)
        W2 = jax.random.uniform(k3, (H, D), jnp.float32, -s2, s2)
        b2 = jnp.zeros((D,), jnp.float32)
        return {'x_all': x_all, 'max_iter': 10, 'ix': 0, 'edge_index': edge_index, 'aug_loss': 0, 'W1': W1, 'b1': b1, 'W2': W2, 'b2': b2}
    _L1_gnn_all = _L1_gnn_setup()
    _L1_gnn_in = {k: v for k, v in _L1_gnn_all.items() if k in ('W1', 'b1', 'W2', 'b2')}
    del _L1_gnn_all
    return {'x': x, 'src': src, 'dst': dst, 'L0_gnn_W': _L0_gnn_in['W'], 'L0_gnn_b': _L0_gnn_in['b'], 'L0_gnn_diffusion_weights': _L0_gnn_in['diffusion_weights'], 'L1_gnn_W1': _L1_gnn_in['W1'], 'L1_gnn_b1': _L1_gnn_in['b1'], 'L1_gnn_W2': _L1_gnn_in['W2'], 'L1_gnn_b2': _L1_gnn_in['b2']}

def reference(x, src, dst, L0_gnn_W, L0_gnn_b, L0_gnn_diffusion_weights, L1_gnn_W1, L1_gnn_b1, L1_gnn_W2, L1_gnn_b2):
    import jax
    import jax.numpy as jnp

    def _L0_gnn_ref(x, edge_index, W, b, diffusion_weights):
        import jax, jax.numpy as jnp
        import numpy as np
        N = 256
        D = 512
        E = 8192
        STEPS = 3
        h = x @ W + b
        row, col = (edge_index[0], edge_index[1])
        adj = jnp.zeros((N, N), dtype=h.dtype)
        adj = adj.at[row, col].set(1.0)
        adj = adj.at[col, row].set(1.0)
        adj = adj + jnp.eye(N, dtype=h.dtype)
        row_sum = adj.sum(axis=1, keepdims=True)
        adj = adj / jnp.maximum(row_sum, 1.0)
        out = diffusion_weights[0] * h
        cur = h
        for i in range(STEPS):
            cur = adj @ cur
            out = out + diffusion_weights[i + 1] * cur
        return jax.nn.relu(out)

    def _L1_gnn_ref(x_all, max_iter, ix, edge_index, aug_loss, W1, b1, W2, b2):
        import jax, jax.numpy as jnp
        import numpy as np
        N = 10000
        D = 512
        H = 4 * D
        E = 5000
        K = 8
        DELTA = D // K

        def _gcn_conv(x, W, b, src, dst, norm, n):
            msgs = x[src] * norm[:, None]
            agg = jax.ops.segment_sum(msgs, dst, num_segments=n)
            return agg @ W + b
        n = x_all.shape[0]
        loop = jnp.arange(n, dtype=edge_index.dtype)
        src = jnp.concatenate([edge_index[0], loop])
        dst = jnp.concatenate([edge_index[1], loop])
        deg = jax.ops.segment_sum(jnp.ones_like(src, dtype=x_all.dtype), dst, num_segments=n)
        dinv = jnp.where(deg > 0, jax.lax.rsqrt(deg), 0.0)
        norm = dinv[src] * dinv[dst]
        x = _gcn_conv(x_all, W1, b1, src, dst, norm, n)
        z = jax.nn.relu(x)
        z = _gcn_conv(z, W2, b2, src, dst, norm, n)
        zk = z.reshape(n, K, DELTA)
        nrm = jnp.sqrt(jnp.sum(zk * zk, axis=2, keepdims=True))
        zk = zk / jnp.maximum(nrm, 1e-12)
        return zk.reshape(n, D)
    edge_index = jnp.stack([src, dst])
    h = jnp.maximum(_layernorm(x, axis=-1), 0.0)
    x = x + _L0_gnn_ref(h, edge_index, L0_gnn_W, L0_gnn_b, L0_gnn_diffusion_weights)
    h = jnp.maximum(_layernorm(x, axis=-1), 0.0)
    x = x + _L1_gnn_ref(h, 10, 0, edge_index, 0, L1_gnn_W1, L1_gnn_b1, L1_gnn_W2, L1_gnn_b2)
    return x

_drawn_inputs = setup_inputs


def setup_inputs(seed=0):
    import zlib

    import numpy as np

    out = dict(_drawn_inputs(seed))
    spreads = {'L0_gnn_b': (0.0, 0.1),
     'L0_gnn_diffusion_weights': (0.25, 0.6),
     'L1_gnn_b1': (0.0, 0.1),
     'L1_gnn_b2': (0.0, 0.1)}
    factors = {}
    for name, (base, spread) in spreads.items():
        noise = np.random.default_rng([zlib.crc32(name.encode()), seed]).standard_normal(out[name].shape)
        drawn = base * np.exp(spread * noise) if base else spread * noise
        out[name] = jnp.asarray(drawn.astype(out[name].dtype))
    for name, factor in factors.items():
        out[name] = (out[name] * factor).astype(out[name].dtype)
    return out
```

```python
from contextlib import ExitStack

import concourse.bass as bass
from concourse import mybir

F32 = mybir.dt.float32
F32R = mybir.dt.float32r
BF16 = mybir.dt.bfloat16
I32 = mybir.dt.int32
ALU = mybir.AluOpType
ACT = mybir.ActivationFunctionType
AX = mybir.AxisListType

P = 128
EPS = 1e-5
NORM_FLOOR = 1e-12
GROUP = 64


def gnn_block(nc, x, src, dst, w, b, dw, w1, b1, w2, b2, out):
    N, D = x.shape
    E = src.shape[0]
    H = w1.shape[1]
    NT = N // P
    DT = D // P
    HT = H // P
    ET = E // P
    NG = D // GROUP
    UNIT = DT * D
    UPM = H // D
    PER = D // P
    ONEHOTS = 6
    ZR = 3

    UNITS = 1 + 2 * UPM
    RAW = 3
    SLOTS = UNITS - 2
    slot = [u if u < SLOTS else u - SLOTS for u in range(UNITS)]

    with ExitStack() as ctx:
        def sb(name, shape, dt=F32):
            return ctx.enter_context(nc.sbuf_tensor(name, shape, dt))

        def sem(name):
            return ctx.enter_context(nc.semaphore(name))

        raw = sb("raw", [P, RAW, DT, D])
        wt_hi = sb("wt_hi", [P, SLOTS, DT, D], F32R)
        wt_lo = sb("wt_lo", [P, SLOTS, DT, D], F32R)
        x_sb = sb("x_sb", [P, NT, D])
        work = sb("work", [P, NT, D])
        temp = sb("temp", [P, NT, D])
        feat_hi = sb("feat_hi", [P, DT, N], F32R)
        feat_lo = sb("feat_lo", [P, DT, N], F32R)
        node_hi = sb("node_hi", [P, NT, D], F32R)
        node_lo = sb("node_lo", [P, NT, D], F32R)
        z_sb = sb("z_sb", [P, ZR, N])
        z_hi = sb("z_hi", [P, ZR, N], F32R)
        z_lo = sb("z_lo", [P, ZR, N], F32R)
        oh_src = sb("oh_src", [P, ONEHOTS, N], BF16)
        oh_dst = sb("oh_dst", [P, ONEHOTS, N], BF16)
        count_t = sb("count_t", [P, NT, N])
        both = sb("both", [P, NT, N])
        m_t = sb("m_t", [P, NT, N], F32R)
        s_adj = sb("s_adj", [P, NT, N], F32R)
        poly_hi = sb("poly_hi", [P, NT, N], F32R)
        poly_lo = sb("poly_lo", [P, NT, N], F32R)
        b_hi = sb("b_hi", [P, NT, N], F32R)
        b_lo = sb("b_lo", [P, NT, N], F32R)
        column = sb("column", [P, N], BF16)
        row = sb("row", [P, NT])
        eye = sb("eye", [P, NT, N])
        ones_r = sb("ones_r", [P, P], F32R)
        wi_hi = sb("wi_hi", [P, 2, P], F32R)
        wi_lo = sb("wi_lo", [P, 2, P], F32R)
        edge_i = sb("edge_i", [P, 2, ET], I32)
        edge_f = sb("edge_f", [P, 2, ET])
        bias0 = temp[0:1, 0, :]
        bias0_hi = b_hi[0:1].rearrange("p t n -> p (t n)")
        bias0_lo = b_lo[0:1].rearrange("p t n -> p (t n)")
        bias1_rows = sb("bias1_rows", [HT, P])
        bias1 = sb("bias1", [P, HT])
        bias2 = sb("bias2", [P, D])
        dw_sb = sb("dw_sb", [P, 4])
        stats = sb("stats", [P, NT, 6])
        mean_var = sb("mean_var", [P, NT, 2])
        var_eps = sb("var_eps", [P, NT])
        minus_half = sb("minus_half", [P, NT])
        rstd = sb("rstd", [P, NT])
        shift = sb("shift", [P, NT])
        stats2 = sb("stats2", [P, NT, 6])
        mean_var2 = sb("mean_var2", [P, NT, 2])
        small = sb("small", [P, NT, 6])
        scale2 = sb("scale2", [P, NT])
        shift2 = sb("shift2", [P, NT])
        row_sum = sb("row_sum", [P, NT])
        r_inv = sb("r_inv", [P, NT])
        r_w3 = sb("r_w3", [P, NT])
        deg = sb("deg", [P, NT])
        dinv = sb("dinv", [P, NT])
        dinv_eye = sb("dinv_eye", [P, NT, P])
        dinv_row = sb("dinv_row", [P, N])
        norm = sb("norm", [P, NT, 5, NG])
        ps = [ctx.enter_context(nc.psum_tensor(f"bank{i}", [P, 512], F32)) for i in range(8)]

        ps_count = [ps[0], ps[1]]
        ps_h0t = [ps[2], ps[3]]
        ps_bias1 = ps[6][:, 0:HT]
        ps_q = [ps[4], ps[5]]
        ps_tr = [ps[6], ps[7]]
        ps_kp = [ps[2], ps[3]]
        ps_b = [ps[0], ps[1]]
        ps_deg = [ps[2][:, 384:386], ps[3][:, 384:386]]
        ps_dinv = ps[2][:, 0:N]
        ps_bq = [ps[6], ps[7]]
        ps_agg = [ps[0], ps[1], ps[2], ps[3]]
        ps_z = [ps[6], ps[7], ps[0]]
        ps_v = [ps[4], ps[5]]
        ps_out = [ps[2], ps[3]]
        ident = eye[:, 0, 0:P]

        edges_in, dw_in, bias0_in, bias1_in, bias2_in = (
            sem(n) for n in ("edges_in", "dw_in", "bias0_in", "bias1_in", "bias2_in"))
        x_in = [sem(f"x_in{t}") for t in range(NT)]
        unit_in = [sem(f"unit_in{u}") for u in range(UNITS)]
        stored = sem("stored")
        iota_done, consts_done, rstd_done, dinv_done, m_t_done, bias0_lo_done = (
            sem(n) for n in ("iota_done", "consts_done", "rstd_done", "dinv_done", "m_t_done", "bias0_lo_done"))
        hi_done = [sem(f"hi_done{u}") for u in range(UNITS)]
        lo_done = [sem(f"lo_done{u}") for u in range(UNITS)]
        h0_done, bias0_hi_done, bias1_done, h0t_hi_done, count_t_done, wi_hi_done = (
            sem(n) for n in ("h0_done", "bias0_hi_done", "bias1_done", "h0t_hi_done", "count_t_done", "wi_hi_done"))
        poly_hi_done, b_hi_done, q_hi_done, w0q_done, dinv_row_done = (
            sem(n) for n in ("poly_hi_done", "b_hi_done", "q_hi_done", "w0q_done", "dinv_row_done"))
        root2_done, h1_hi_done, agg_hi_done, z_done, v_hi_done, square_done, root3_done = (
            sem(n) for n in ("root2_done", "h1_hi_done", "agg_hi_done", "z_done", "v_hi_done", "square_done",
                             "root3_done"))
        eye_done, var_done, shift_done, onehot_done, h0t_lo_done, s_done, r_done = (
            sem(n) for n in ("eye_done", "var_done", "shift_done", "onehot_done", "h0t_lo_done", "s_done", "r_done"))
        wi_lo_done, poly_lo_done, b_lo_done, q_lo_done, deg_done, dinv_eye_done = (
            sem(n) for n in ("wi_lo_done", "poly_lo_done", "b_lo_done", "q_lo_done", "deg_done", "dinv_eye_done"))
        x1_done, var2_done, scale2_done, h1_lo_done, agg_done, agg_lo_done = (
            sem(n) for n in ("x1_done", "var2_done", "scale2_done", "h1_lo_done", "agg_done", "agg_lo_done"))
        z_hi_done, z_lo_done, v_lo_done, v_done, sum_done, out_done, dve_own = (
            sem(n) for n in ("z_hi_done", "z_lo_done", "v_lo_done", "v_done", "sum_done", "out_done", "dve_own"))
        counted, h0t_ps_done, bias1_ps_done, tr_ps_done, kp_ps_done, b_ps_done, q_ps_done = (
            sem(n) for n in ("counted", "h0t_ps_done", "bias1_ps_done", "tr_ps_done", "kp_ps_done", "b_ps_done",
                             "q_ps_done"))
        deg_ps_done, dinv_ps_done, bq_ps_done, agg_ps_done, z_ps_done, z_used, v_ps_done, out_ps_done = (
            sem(n) for n in ("deg_ps_done", "dinv_ps_done", "bq_ps_done", "agg_ps_done", "z_ps_done", "z_used",
                             "v_ps_done", "out_ps_done"))

        w_rows = w.rearrange("(c p) n -> p c n", p=P)
        w1_rows = w1.rearrange("(c p) (u n) -> u p c n", p=P, n=D)
        w2_rows = w2.rearrange("(u c p) n -> u p c n", p=P, c=DT)
        x_rows = x.rearrange("(t p) d -> t p d", p=P)
        out_rows = out.rearrange("(t p) d -> t p d", p=P)

        def unit_dram(u):
            return w_rows if u == 0 else w1_rows[u - 1] if u <= UPM else w2_rows[u - 1 - UPM]

        def w_part(part, c):
            return part[:, slot[0], c, :]

        def w1_part(part, c, j):
            return part[:, slot[1 + j // PER], c, (j % PER) * P:(j % PER + 1) * P]

        def w2_part(part, j):
            return part[:, slot[1 + UPM + j // PER], j % PER, :]

        def work_feat(c):
            return work[:].rearrange("p t d -> p (t d)")[:, c * N:(c + 1) * N]

        def split_waits(eng, u, part_done):
            if u == UNITS - 2:
                eng.wait_ge(q_ps_done, NT)
            if u == UNITS - 1:
                eng.wait_ge(z_ps_done, PER)

        block = ctx.enter_context(nc.Block())

        @block.sync
        def _(sp):
            sp.dma_start(edge_i[:, 0, :], src.rearrange("(p t) -> p t", t=ET)).then_inc(edges_in, 16)
            sp.dma_start(edge_i[:, 1, :], dst.rearrange("(p t) -> p t", t=ET)).then_inc(edges_in, 16)
            for t in range(NT):
                sp.dma_start(x_sb[:, t, :], x_rows[t]).then_inc(x_in[t], 16)
            for u in range(UNITS):
                if u >= RAW:
                    sp.wait_ge(hi_done[u - RAW], DT)
                    sp.wait_ge(lo_done[u - RAW], DT)
                sp.dma_start(raw[:, u % RAW], unit_dram(u)).then_inc(unit_in[u], 16)
            for t in range(NT):
                sp.wait_ge(out_done, t + 1)
                sp.dma_start(out_rows[t], work[:, t, :]).then_inc(stored, 16)
            sp.wait_ge(stored, 16 * NT)

        @block.gpsimd
        def _(pool):
            nc.gpsimd.iota(column[:], [[1, N]], base=0, channel_multiplier=0,
                           allow_small_or_imprecise_dtypes=True).then_inc(iota_done, 1)
            nc.gpsimd.iota(row[:], [[P, NT]], base=0, channel_multiplier=1,
                           allow_small_or_imprecise_dtypes=True).then_inc(iota_done, 1)
            nc.gpsimd.memset(minus_half[:], -0.5).then_inc(consts_done, 1)
            nc.gpsimd.memset(ones_r[:].bitcast(F32), 1.0).then_inc(consts_done, 1)
            pool.wait_ge(consts_done, 1)
            pool.wait_ge(var_done, 1)
            nc.gpsimd.tensor_tensor(rstd[:], var_eps[:], minus_half[:], ALU.pow).then_inc(rstd_done, 1)

            def split_lo(u, c):
                pool.wait_ge(hi_done[u], c + 1)
                split_waits(pool, u, lo_done)
                nc.gpsimd.tensor_tensor(wt_lo[:, slot[u], c, :], raw[:, u % RAW, c, :],
                                        wt_hi[:, slot[u], c, :].bitcast(F32), ALU.subtract).then_inc(lo_done[u], 1)

            for c in range(DT):
                split_lo(0, c)
            pool.wait_ge(bias0_hi_done, 1)
            nc.gpsimd.tensor_tensor(bias0_lo, bias0, bias0_hi.bitcast(F32),
                                    ALU.subtract).then_inc(bias0_lo_done, 1)
            pool.wait_ge(eye_done, NT)
            for t in range(NT):
                pool.wait_ge(count_t_done, t + 1)
                nc.gpsimd.tensor_tensor(m_t[:, t, :], count_t[:, t, :], eye[:, t, :], ALU.add).then_inc(m_t_done, 1)
            pool.wait_ge(deg_done, NT)
            nc.gpsimd.tensor_tensor(dinv[:], deg[:], minus_half[:], ALU.pow).then_inc(dinv_done, 1)
            for u in range(1 + UPM, UNITS):
                for c in range(DT):
                    split_lo(u, c)

        @block.scalar
        def _(act):
            act.dma_start(dw_sb[:], dw.partition_broadcast(P)).then_inc(dw_in, 16)
            act.dma_start(bias0, b.rearrange("(o k) -> o k", o=1)).then_inc(bias0_in, 16)
            act.dma_start(bias1_rows[:], b1.rearrange("(j p) -> j p", p=P)).then_inc(bias1_in, 16)
            act.dma_start(bias2[:], b2.partition_broadcast(P)).then_inc(bias2_in, 16)

            def split_hi(u, c):
                if c == 0:
                    act.wait_ge(unit_in[u], 16)
                    split_waits(act, u, hi_done)
                nc.scalar.activation(wt_hi[:, slot[u], c, :], raw[:, u % RAW, c, :], ACT.Copy).then_inc(hi_done[u], 1)

            act.wait_ge(shift_done, 1)
            for t in range(NT):
                nc.scalar.activation(work[:, t, :], x_sb[:, t, :], ACT.Relu, bias=shift[:, t:t + 1],
                                     scale=rstd[:, t:t + 1]).then_inc(h0_done, 1)
            for c in range(DT):
                split_hi(0, c)
            act.wait_ge(bias0_in, 16)
            nc.scalar.activation(bias0_hi, bias0, ACT.Copy).then_inc(bias0_hi_done, 1)
            for t in range(2):
                act.wait_ge(h0t_ps_done, t + 1)
                nc.scalar.activation(feat_hi[:, 2 * t:2 * t + 2, :], ps_h0t[t][:].rearrange("p (c n) -> p c n", n=N),
                                     ACT.Copy).then_inc(h0t_hi_done, 1)
            act.wait_ge(dw_in, 16)
            act.wait_ge(eye_done, NT)
            for k in range(2):
                nc.scalar.activation(wi_hi[:, k, :], ident, ACT.Copy, scale=dw_sb[:, k + 1:k + 2]).then_inc(wi_hi_done, 1)
            act.wait_ge(bias1_ps_done, 1)
            nc.scalar.activation(bias1[:], ps_bias1, ACT.Copy).then_inc(bias1_done, 1)
            for c in range(3):
                split_hi(1, c)
            for t in range(NT):
                act.wait_ge(counted, ET)
                nc.scalar.activation(count_t[:, t, :], ps_count[t][:, 0:N], ACT.Copy).then_inc(count_t_done, 1)
            split_hi(1, 3)
            for t in range(NT):
                act.wait_ge(r_done, t + 1)
                nc.scalar.activation(poly_hi[:, t, :], s_adj[:, t, :].bitcast(F32), ACT.Copy,
                                     scale=r_w3[:, t:t + 1]).then_inc(poly_hi_done, 1)

            def q_parts(t):
                act.wait_ge(q_ps_done, t + 1)
                nc.scalar.activation(node_hi[:, t, :], ps_q[t][:], ACT.Copy).then_inc(q_hi_done, 1)
                nc.scalar.activation(work[:, t, :], ps_q[t][:], ACT.Copy, scale=dw_sb[:, 0:1]).then_inc(w0q_done, 1)

            q_parts(0)
            for t in range(NT):
                act.wait_ge(kp_ps_done, t + 1)
                nc.scalar.activation(poly_hi[:, t, :], ps_kp[t][:, 0:N], ACT.Copy,
                                     scale=r_inv[:, t:t + 1]).then_inc(poly_hi_done, 1)
            for c in range(DT):
                split_hi(2, c)
            for t in range(NT):
                act.wait_ge(b_ps_done, t + 1)
                nc.scalar.activation(b_hi[:, t, :], ps_b[t][:, 0:N], ACT.Copy).then_inc(b_hi_done, 1)
            q_parts(1)
            act.wait_ge(dinv_ps_done, 1)
            nc.scalar.activation(dinv_row[:], ps_dinv, ACT.Copy).then_inc(dinv_row_done, 1)
            for c in range(DT):
                split_hi(3, c)
            for t in range(NT):
                act.wait_ge(var2_done, t + 1)
                nc.scalar.activation(small[:, t, 1:2], small[:, t, 0:1], ACT.Sqrt).then_inc(root2_done, 1)
                act.wait_ge(scale2_done, t + 1)
                act.wait_ge(bq_ps_done, NT)
                nc.scalar.activation(node_hi[:, t, :], x_sb[:, t, :], ACT.Relu, bias=shift2[:, t:t + 1],
                                     scale=scale2[:, t:t + 1]).then_inc(h1_hi_done, 1)
            for c in range(DT):
                act.wait_ge(agg_done, c + 1)
                nc.scalar.activation(feat_hi[:, c, :], work_feat(c), ACT.Copy).then_inc(agg_hi_done, 1)
            hi_left = [(u, c) for u in range(UPM, UNITS) for c in range(DT)]
            for j in range(HT):
                act.wait_ge(z_ps_done, j + 1)
                if j >= ZR:
                    act.wait_ge(z_lo_done, j - ZR + 1)
                if j == 0:
                    act.wait_ge(bias1_done, 1)
                nc.scalar.activation(z_sb[:, j % ZR, :], ps_z[j % ZR][:, 0:N], ACT.Relu,
                                     bias=bias1[:, j:j + 1]).then_inc(z_done, 1)
                for _ in range(2 if j < 5 else 1):
                    if hi_left and hi_left[0][0] < UNITS - 1 or (hi_left and j >= PER):
                        split_hi(*hi_left.pop(0))
            for t in range(NT):
                act.wait_ge(v_ps_done, t + 1)
                nc.scalar.activation(node_hi[:, t, :], ps_v[t][:], ACT.Copy, scale=dinv[:, t:t + 1]).then_inc(v_hi_done, 1)
            for t in range(NT):
                act.wait_ge(v_done, t + 1)
                nc.scalar.activation(temp[:, t, :], work[:, t, :], ACT.Square).then_inc(square_done, 1)
            for t in range(NT):
                act.wait_ge(sum_done, t + 1)
                nc.scalar.activation(norm[:, t, 1, :], norm[:, t, 0, :], ACT.Sqrt).then_inc(root3_done, 1)

        @block.vector
        def _(dve):
            own = [0]

            def mine(ins):
                own[0] += 1
                ins.then_inc(dve_own, 1)
                return own[0]

            def after(ins):
                dve.wait_ge(dve_own, mine(ins))

            def split_lo(u, c):
                dve.wait_ge(hi_done[u], c + 1)
                nc.vector.tensor_tensor(wt_lo[:, slot[u], c, :], raw[:, u % RAW, c, :],
                                        wt_hi[:, slot[u], c, :].bitcast(F32), ALU.subtract).then_inc(lo_done[u], 1)

            dve.wait_ge(iota_done, 2)
            for t in range(NT):
                nc.vector.tensor_scalar(eye[:, t, :], column[:], row[:, t:t + 1], None, ALU.is_equal).then_inc(eye_done, 1)
            dve.wait_ge(edges_in, 32)
            after(nc.vector.tensor_copy(edge_f[:], edge_i[:]))

            def onehot(t):
                if t >= ONEHOTS:
                    dve.wait_ge(counted, t - ONEHOTS + 1)
                nc.vector.tensor_scalar(oh_src[:, t % ONEHOTS, :], column[:], edge_f[:, 0, t:t + 1], None, ALU.is_equal)
                nc.vector.tensor_scalar(oh_dst[:, t % ONEHOTS, :], column[:], edge_f[:, 1, t:t + 1], None,
                                        ALU.is_equal).then_inc(onehot_done, 1)

            for t in range(ET):
                onehot(t)
                if t in (4, 5):
                    dve.wait_ge(x_in[t - 4], 16)
                    n_stats = mine(nc.vector.bn_stats(stats[:, t - 4, :], x_sb[:, t - 4, :]))
                if t in (6, 7):
                    dve.wait_ge(dve_own, n_stats)
                    n_aggr = mine(nc.vector.bn_aggr(mean_var[:, t - 6, :], stats[:, t - 6, :]))
                if t == 8:
                    dve.wait_ge(dve_own, n_aggr)
                    nc.vector.tensor_scalar(var_eps[:], mean_var[:, :, 1], EPS, None, ALU.add).then_inc(var_done, 1)
                if t == 12:
                    dve.wait_ge(rstd_done, 1)
                    nc.vector.scalar_tensor_tensor(out=shift[:], in0=mean_var[:, :, 0], scalar=-1.0, in1=rstd[:],
                                                   op0=ALU.mult, op1=ALU.mult).then_inc(shift_done, 1)
                if t in (26, 28):
                    k = (t - 26) // 2
                    dve.wait_ge(h0t_hi_done, k + 1)
                    nc.vector.tensor_tensor(feat_lo[:, 2 * k:2 * k + 2, :], ps_h0t[k][:].rearrange("p (c n) -> p c n", n=N),
                                            feat_hi[:, 2 * k:2 * k + 2, :].bitcast(F32), ALU.subtract).then_inc(h0t_lo_done, 1)
                if t == 30:
                    for k in range(2):
                        dve.wait_ge(wi_hi_done, k + 1)
                        nc.vector.scalar_tensor_tensor(out=wi_lo[:, k, :], in0=ident, scalar=dw_sb[:, k + 1:k + 2],
                                                       in1=wi_hi[:, k, :].bitcast(F32), op0=ALU.mult,
                                                       op1=ALU.subtract).then_inc(wi_lo_done, 1)
            for t in range(NT):
                dve.wait_ge(tr_ps_done, t + 1)
                dve.wait_ge(count_t_done, t + 1)
                after(nc.vector.tensor_tensor(both[:, t, :], ps_tr[t][:, 0:N], count_t[:, t, :], ALU.add))
                ins = nc.vector.scalar_tensor_tensor(out=s_adj[:, t, :], in0=both[:, t, :], scalar=1.0,
                                                     in1=eye[:, t, :], op0=ALU.min, op1=ALU.add,
                                                     accum_out=row_sum[:, t:t + 1])
                ins.then_inc(s_done, 1)
                dve.wait_ge(s_done, t + 1)
                after(nc.vector.tensor_scalar(row_sum[:, t:t + 1], row_sum[:, t:t + 1], 1.0, None, ALU.max))
                after(nc.vector.reciprocal(r_inv[:, t:t + 1], row_sum[:, t:t + 1]))
                nc.vector.tensor_tensor(r_w3[:, t:t + 1], r_inv[:, t:t + 1], dw_sb[:, 3:4], ALU.mult).then_inc(r_done, 1)
            for t in range(NT):
                dve.wait_ge(poly_hi_done, t + 1)
                dve.wait_ge(r_done, t + 1)
                nc.vector.scalar_tensor_tensor(out=poly_lo[:, t, :], in0=s_adj[:, t, :].bitcast(F32),
                                               scalar=r_w3[:, t:t + 1], in1=poly_hi[:, t, :].bitcast(F32),
                                               op0=ALU.mult, op1=ALU.subtract).then_inc(poly_lo_done, 1)

            def q_lo(t):
                dve.wait_ge(q_hi_done, t + 1)
                dve.wait_ge(w0q_done, t + 1)
                nc.vector.tensor_tensor(node_lo[:, t, :], ps_q[t][:], node_hi[:, t, :].bitcast(F32),
                                        ALU.subtract).then_inc(q_lo_done, 1)

            for c in range(2):
                split_lo(1, c)
            q_lo(0)
            for t in range(NT):
                dve.wait_ge(poly_hi_done, NT + t + 1)
                nc.vector.scalar_tensor_tensor(out=poly_lo[:, t, :], in0=ps_kp[t][:, 0:N], scalar=r_inv[:, t:t + 1],
                                               in1=poly_hi[:, t, :].bitcast(F32), op0=ALU.mult,
                                               op1=ALU.subtract).then_inc(poly_lo_done, 1)
            for t in range(NT):
                dve.wait_ge(deg_ps_done, t + 1)
                nc.vector.tensor_copy(deg[:, t:t + 1], ps_deg[t][:, 0:1]).then_inc(deg_done, 1)
            for t in range(NT):
                dve.wait_ge(b_hi_done, t + 1)
                nc.vector.tensor_tensor(b_lo[:, t, :], ps_b[t][:, 0:N], b_hi[:, t, :].bitcast(F32),
                                        ALU.subtract).then_inc(b_lo_done, 1)
            q_lo(1)
            for t in range(NT):
                dve.wait_ge(dinv_done, 1)
                nc.vector.tensor_scalar(dinv_eye[:, t, :], ident, dinv[:, t:t + 1], None, ALU.mult).then_inc(dinv_eye_done, 1)
            for c in range(2, DT):
                split_lo(1, c)
            for c in range(DT):
                split_lo(2, c)

            def x1_and_stats(t):
                dve.wait_ge(bq_ps_done, t + 1)
                dve.wait_ge(w0q_done, t + 1)
                after(nc.vector.scalar_tensor_tensor(out=temp[:, t, :], in0=ps_bq[t][:], scalar=r_inv[:, t:t + 1],
                                                     in1=work[:, t, :], op0=ALU.mult, op1=ALU.add))
                ins = nc.vector.scalar_tensor_tensor(out=x_sb[:, t, :], in0=temp[:, t, :], scalar=0.0,
                                                     in1=x_sb[:, t, :], op0=ALU.max, op1=ALU.add)
                ins.then_inc(x1_done, 1)
                dve.wait_ge(x1_done, t + 1)
                after(nc.vector.bn_stats(stats2[:, t, :], x_sb[:, t, :]))
                after(nc.vector.bn_aggr(mean_var2[:, t, :], stats2[:, t, :]))
                ins = nc.vector.tensor_scalar(small[:, t, 0:1], mean_var2[:, t, 1:2], EPS, None, ALU.add)
                ins.then_inc(var2_done, 1)

            def h1_parts(t):
                dve.wait_ge(root2_done, t + 1)
                after(nc.vector.reciprocal(small[:, t, 2:3], small[:, t, 1:2]))
                dve.wait_ge(var2_done, t + 1)
                after(nc.vector.scalar_tensor_tensor(out=small[:, t, 3:4], in0=small[:, t, 0:1],
                                                     scalar=small[:, t, 2:3], in1=small[:, t, 2:3],
                                                     op0=ALU.mult, op1=ALU.mult))
                after(nc.vector.tensor_scalar(small[:, t, 4:5], small[:, t, 3:4], -0.5, 1.5, ALU.mult, ALU.add))
                after(nc.vector.scalar_tensor_tensor(out=scale2[:, t:t + 1], in0=small[:, t, 4:5],
                                                     scalar=small[:, t, 2:3], in1=dinv[:, t:t + 1],
                                                     op0=ALU.mult, op1=ALU.mult))
                after(nc.vector.scalar_tensor_tensor(out=shift2[:, t:t + 1], in0=mean_var2[:, t, 0:1], scalar=-1.0,
                                                     in1=scale2[:, t:t + 1], op0=ALU.mult, op1=ALU.mult))
                nc.vector.tensor_scalar(temp[:, t, :], x_sb[:, t, :], scale2[:, t:t + 1], shift2[:, t:t + 1],
                                        ALU.mult, ALU.add).then_inc(scale2_done, 1)
                dve.wait_ge(scale2_done, t + 1)
                dve.wait_ge(h1_hi_done, t + 1)
                nc.vector.scalar_tensor_tensor(out=node_lo[:, t, :], in0=temp[:, t, :], scalar=0.0,
                                               in1=node_hi[:, t, :].bitcast(F32), op0=ALU.max,
                                               op1=ALU.subtract).then_inc(h1_lo_done, 1)

            for t in range(NT):
                x1_and_stats(t)
                h1_parts(t)

            dve.wait_ge(dinv_row_done, 1)
            for c in range(DT):
                dve.wait_ge(agg_ps_done, c + 1)
                dve.wait_ge(x1_done, NT)
                nc.vector.tensor_tensor(work_feat(c), ps_agg[c][:, 0:N], dinv_row[:], ALU.mult).then_inc(agg_done, 1)
                if c >= 1:
                    dve.wait_ge(agg_hi_done, c)
                    nc.vector.tensor_tensor(feat_lo[:, c - 1, :], work_feat(c - 1), feat_hi[:, c - 1, :].bitcast(F32),
                                            ALU.subtract).then_inc(agg_lo_done, 1)
            dve.wait_ge(agg_hi_done, DT)
            nc.vector.tensor_tensor(feat_lo[:, DT - 1, :], work_feat(DT - 1), feat_hi[:, DT - 1, :].bitcast(F32),
                                    ALU.subtract).then_inc(agg_lo_done, 1)
            lo_left = [(u, c) for u in range(3, 1 + UPM) for c in range(DT)]
            for j in range(HT):
                dve.wait_ge(z_done, j + 1)
                if j >= ZR:
                    dve.wait_ge(z_used, j - ZR + 1)
                nc.vector.tensor_copy(z_hi[:, j % ZR, :], z_sb[:, j % ZR, :]).then_inc(z_hi_done, 1)
                dve.wait_ge(z_hi_done, j + 1)
                nc.vector.tensor_tensor(z_lo[:, j % ZR, :], z_sb[:, j % ZR, :], z_hi[:, j % ZR, :].bitcast(F32),
                                        ALU.subtract).then_inc(z_lo_done, 1)
                for _ in range(2):
                    if lo_left:
                        split_lo(*lo_left.pop(0))
            for t in range(NT):
                dve.wait_ge(v_hi_done, t + 1)
                nc.vector.scalar_tensor_tensor(out=node_lo[:, t, :], in0=ps_v[t][:], scalar=dinv[:, t:t + 1],
                                               in1=node_hi[:, t, :].bitcast(F32), op0=ALU.mult,
                                               op1=ALU.subtract).then_inc(v_lo_done, 1)
            dve.wait_ge(bias2_in, 16)
            for t in range(NT):
                dve.wait_ge(out_ps_done, t + 1)
                nc.vector.scalar_tensor_tensor(out=work[:, t, :], in0=ps_out[t][:], scalar=dinv[:, t:t + 1],
                                               in1=bias2[:], op0=ALU.mult, op1=ALU.add).then_inc(v_done, 1)
            for t in range(NT):
                dve.wait_ge(square_done, t + 1)
                nc.vector.tensor_reduce(norm[:, t, 0, :], temp[:, t, :].rearrange("p (g k) -> p g k", k=GROUP),
                                        AX.X, ALU.add).then_inc(sum_done, 1)
            for t in range(NT):
                total, root, inv, aux, step = (norm[:, t, k, :] for k in range(5))
                dve.wait_ge(root3_done, t + 1)
                after(nc.vector.tensor_scalar(step, root, 1e-8 * NORM_FLOOR, None, ALU.max))
                after(nc.vector.reciprocal(inv, step))
                dve.wait_ge(sum_done, t + 1)
                after(nc.vector.tensor_tensor(aux, total, inv, ALU.mult))
                after(nc.vector.tensor_tensor(root, aux, inv, ALU.mult))
                after(nc.vector.tensor_scalar(step, root, -0.5, 1.5, ALU.mult, ALU.add))
                after(nc.vector.tensor_tensor(aux, step, inv, ALU.mult))
                after(nc.vector.tensor_scalar(inv, aux, 1.0 / NORM_FLOOR, None, ALU.min))
                v_groups = work[:, t, :].rearrange("p (g k) -> p g k", k=GROUP)
                after(nc.vector.tensor_tensor(temp[:, t, :].rearrange("p (g k) -> p g k", k=GROUP), v_groups,
                                              inv.unsqueeze(2).broadcast_to([P, NG, GROUP]), ALU.mult))
                nc.vector.tensor_tensor(work[:, t, :], temp[:, t, :], x_sb[:, t, :], ALU.add).then_inc(out_done, 1)

        @block.tensor
        def _(pe):
            def product(bank, terms, done=None, start=True, stop=True):
                for i, (stationary, moving) in enumerate(terms):
                    last = nc.tensor.matmul(bank, stationary, moving, start=start and i == 0,
                                            stop=stop and i == len(terms) - 1)
                if done is not None:
                    last.then_inc(done, 1)

            for t in range(ET):
                pe.wait_ge(onehot_done, t + 1)
                for s in range(NT):
                    last = nc.tensor.matmul(ps_count[s][:, 0:N], oh_src[:, t % ONEHOTS, s * P:(s + 1) * P],
                                            oh_dst[:, t % ONEHOTS, :], start=t == 0, stop=t == ET - 1)
                last.then_inc(counted, 1)
                if t == 16:
                    pe.wait_ge(eye_done, NT)
                    pe.wait_ge(bias1_in, 16)
                    nc.tensor.transpose(ps_bias1, bias1_rows[:], ident[0:HT, 0:HT]).then_inc(bias1_ps_done, 1)
                if t in (20, 21):
                    k = t - 20
                    pe.wait_ge(h0_done, NT)
                    for c in (2 * k, 2 * k + 1):
                        for n in range(NT):
                            at = (c % 2) * N + n * P
                            last = nc.tensor.transpose(ps_h0t[k][:, at:at + P], work[:, n, c * P:(c + 1) * P], ident)
                    last.then_inc(h0t_ps_done, 1)
            pe.wait_ge(bias1_done, 1)
            pe.wait_ge(count_t_done, NT)
            for t in range(NT):
                for s in range(NT):
                    last = nc.tensor.transpose(ps_tr[t][:, s * P:(s + 1) * P], count_t[:, s, t * P:(t + 1) * P], ident)
                last.then_inc(tr_ps_done, 1)

            def q_terms(t):
                at = slice(t * P, (t + 1) * P)
                terms = [(ones_r[0:1, :], bias0_hi), (ones_r[0:1, :], bias0_lo)]
                for c in range(DT):
                    terms += [(feat_hi[:, c, at], w_part(wt_hi, c)), (feat_lo[:, c, at], w_part(wt_hi, c)),
                              (feat_hi[:, c, at], w_part(wt_lo, c))]
                return terms

            pe.wait_ge(h0t_lo_done, 2)
            pe.wait_ge(lo_done[0], DT)
            pe.wait_ge(consts_done, 2)
            pe.wait_ge(bias0_lo_done, 1)
            product(ps_q[0][:], q_terms(0), q_ps_done)

            def times_s(banks, k, lo_count, done):
                for m in range(NT):
                    at = slice(m * P, (m + 1) * P)
                    first = True
                    for c in range(NT):
                        for part in (wi_hi, wi_lo):
                            nc.tensor.matmul(banks[m][:, c * P:(c + 1) * P], s_adj[:, c, at], part[:, k, :],
                                             start=first, stop=False, skip_group_check=True)
                            first = False
                for c in range(NT):
                    pe.wait_ge(poly_lo_done, lo_count + c + 1)
                    for m in range(NT):
                        at = slice(m * P, (m + 1) * P)
                        for part in (poly_hi, poly_lo):
                            last = nc.tensor.matmul(banks[m][:, 0:N], s_adj[:, c, at], part[:, c, :], start=False,
                                                    stop=c == NT - 1 and part is poly_lo, skip_group_check=True)
                        if c == NT - 1:
                            last.then_inc(done, 1)

            pe.wait_ge(s_done, NT)
            pe.wait_ge(wi_lo_done, 2)
            times_s(ps_kp, 1, 0, kp_ps_done)
            q1 = q_terms(1)
            product(ps_q[1][:], q1[:7], stop=False)
            times_s(ps_b, 0, NT, b_ps_done)
            pe.wait_ge(m_t_done, NT)
            for t in range(NT):
                product(ps_deg[t], [(m_t[:, s, t * P:(t + 1) * P], ones_r[:, 0:2]) for s in range(NT)], deg_ps_done)
            product(ps_q[1][:], q1[7:], q_ps_done, start=False)
            pe.wait_ge(dinv_eye_done, NT)
            for t in range(NT):
                last = nc.tensor.matmul(ps_dinv[:, t * P:(t + 1) * P], ones_r[:].bitcast(F32), dinv_eye[:, t, :], start=True, stop=True)
            last.then_inc(dinv_ps_done, 1)
            pe.wait_ge(b_lo_done, NT)
            pe.wait_ge(q_lo_done, NT)
            for t in range(NT):
                at = slice(t * P, (t + 1) * P)
                product(ps_bq[t][:], [(l[:, s, at], r[:, s, :]) for s in range(NT)
                                      for l, r in ((b_hi, node_hi), (b_lo, node_hi), (b_hi, node_lo))], bq_ps_done)
            pe.wait_ge(dinv_row_done, 1)
            for s in range(NT):
                pe.wait_ge(h1_lo_done, s + 1)
                for c in range(DT):
                    product(ps_agg[c][:, 0:N], [(part[:, s, c * P:(c + 1) * P], m_t[:, s, :])
                                                for part in (node_hi, node_lo)],
                            agg_ps_done if s == NT - 1 else None, start=s == 0, stop=s == NT - 1)

            def hidden(j):
                pe.wait_ge(lo_done[1 + j // PER], DT)
                if j >= ZR:
                    pe.wait_ge(z_done, j - ZR + 1)
                if j == 0:
                    pe.wait_ge(agg_lo_done, DT)
                product(ps_z[j % ZR][:, 0:N], [(w1_part(l, c, j), r[:, c, :]) for c in range(DT)
                                               for l, r in ((wt_hi, feat_hi), (wt_hi, feat_lo), (wt_lo, feat_hi))],
                        z_ps_done)

            def project(j):
                pe.wait_ge(z_lo_done, j + 1)
                pe.wait_ge(lo_done[1 + UPM + j // PER], j % PER + 1)
                for t in range(NT):
                    at = slice(t * P, (t + 1) * P)
                    product(ps_v[t][:], [(l[:, j % ZR, at], w2_part(r, j))
                                         for l, r in ((z_hi, wt_hi), (z_lo, wt_hi), (z_hi, wt_lo))],
                            v_ps_done if j == HT - 1 else z_used if t == NT - 1 else None, start=j == 0,
                            stop=j == HT - 1)

            LAG = 2
            for j in range(HT + LAG):
                if j < HT:
                    hidden(j)
                if j >= LAG:
                    project(j - LAG)
            for t in range(NT):
                at = slice(t * P, (t + 1) * P)
                pe.wait_ge(v_lo_done, NT)
                product(ps_out[t][:], [(m_t[:, s, at], part[:, s, :]) for s in range(NT)
                                       for part in (node_hi, node_lo)], out_ps_done)


_INS = ['x', 'src', 'dst', 'L0_gnn_W', 'L0_gnn_b', 'L0_gnn_diffusion_weights', 'L1_gnn_W1', 'L1_gnn_b1', 'L1_gnn_W2',
        'L1_gnn_b2']


def kernel(**inputs):
    import numpy as _np
    import concourse.bacc as _bacc
    from concourse import mybir as _mybir
    from concourse.bass_utils import run_bass_kernel_spmd as _run

    nc = _bacc.Bacc("TRN2", target_bir_lowering=False, num_devices=1)
    arrays, args = {}, []
    for name in _INS:
        a = _np.ascontiguousarray(inputs[name])
        arrays[f"in_{name}"] = a
        args.append(nc.dram_tensor(f"in_{name}", a.shape, _mybir.dt.from_np(a.dtype), kind="ExternalInput").ap())
    out = nc.dram_tensor("out", inputs['x'].shape, _mybir.dt.float32, kind="ExternalOutput").ap()
    gnn_block(nc, *args, out)
    r = _run(nc, [arrays], core_ids=[0])
    return r.results[0]["out"]
```

```python
from contextlib import ExitStack

import concourse.bass as bass
from concourse import mybir

F32 = mybir.dt.float32
F32R = mybir.dt.float32r
BF16 = mybir.dt.bfloat16
I32 = mybir.dt.int32
ALU = mybir.AluOpType
ACT = mybir.ActivationFunctionType
AX = mybir.AxisListType

P = 128
EPS = 1e-5
NORM_FLOOR = 1e-12
GROUP = 64
TINY = 1e-30


def gnn_block(nc, x, src, dst, w, b, dw, w1, b1, w2, b2, out):
    N, D = x.shape
    E = src.shape[0]
    H = w1.shape[1]
    NT = N // P
    DT = D // P
    HT = H // P
    ET = E // P
    NG = D // GROUP
    UNIT = DT * D
    UPM = H // D
    PER = D // P
    PAIRS = ET // 2
    assert ET % 2 == 0
    ONEHOTS = 4
    HALF = D // 2
    ZR = 3

    UNITS = 1 + 2 * UPM
    RAW = 3
    SLOTS = UNITS - 2
    slot = [u if u < SLOTS else u - SLOTS for u in range(UNITS)]

    with ExitStack() as ctx:
        def sb(name, shape, dt=F32):
            return ctx.enter_context(nc.sbuf_tensor(name, shape, dt))

        def sem(name):
            return ctx.enter_context(nc.semaphore(name))

        raw = sb("raw", [P, RAW, DT, D])
        wt_hi = sb("wt_hi", [P, SLOTS, DT, D], F32R)
        wt_lo = sb("wt_lo", [P, SLOTS, DT, D], F32R)
        x_sb = sb("x_sb", [P, NT, D])
        work = sb("work", [P, NT, D])
        temp = sb("temp", [P, NT, D])
        feat_hi = sb("feat_hi", [P, DT, N], F32R)
        feat_lo = sb("feat_lo", [P, DT, N], F32R)
        node_hi = sb("node_hi", [P, NT, D], F32R)
        node_lo = sb("node_lo", [P, NT, D], F32R)
        z_sb = sb("z_sb", [P, ZR, N])
        z_hi = sb("z_hi", [P, ZR, N], F32R)
        z_lo = sb("z_lo", [P, ZR, N], F32R)
        onehots = sb("onehots", [P, ONEHOTS, 2, N, 2], BF16)
        count_t = sb("count_t", [P, NT, N])
        both = temp[:, 1, :].rearrange("p (t n) -> p t n", n=N)
        m_t = sb("m_t", [P, NT, N], F32R)
        s_adj = sb("s_adj", [P, NT, N], F32R)
        poly_hi = sb("poly_hi", [P, NT, N], F32R)
        poly_lo = sb("poly_lo", [P, NT, N], F32R)
        b_hi = sb("b_hi", [P, NT, N], F32R)
        b_lo = sb("b_lo", [P, NT, N], F32R)
        column = sb("column", [P, N, 2], BF16)
        row = sb("row", [P, NT])
        eye = sb("eye", [P, NT, N])
        ones_r = sb("ones_r", [P, P], F32R)
        wi_hi = sb("wi_hi", [P, 3, P], F32R)
        wi_lo = sb("wi_lo", [P, 3, P], F32R)
        edge_i = sb("edge_i", [P, 2, ET], I32)
        edge_b = sb("edge_b", [P, 2, ET], BF16)
        ready = sb("ready", [P, 1])
        diag_r = sb("diag_r", [P, NT, P], F32R)
        bias0 = temp[0:1, 0, :]
        bias0_hi = b_hi[0:1].rearrange("p t n -> p (t n)")
        bias0_lo = b_lo[0:1].rearrange("p t n -> p (t n)")
        bias1_rows = sb("bias1_rows", [HT, P])
        bias1 = sb("bias1", [P, HT])
        bias2 = sb("bias2", [P, D])
        dw_sb = sb("dw_sb", [P, 4])
        stats = sb("stats", [P, NT, 6])
        mean_var = sb("mean_var", [P, NT, 2])
        var_eps = sb("var_eps", [P, NT])
        minus_half = sb("minus_half", [P, NT])
        rstd = sb("rstd", [P, NT])
        shift = sb("shift", [P, NT])
        stats2 = sb("stats2", [P, NT, 6])
        mean_var2 = sb("mean_var2", [P, NT, 2])
        var_eps2, root2, inv2, inv2_dinv, newton_a, newton_b, scale2, shift2 = (
            sb(n, [P, NT]) for n in ("var_eps2", "root2", "inv2", "inv2_dinv", "newton_a", "newton_b", "scale2",
                                     "shift2"))
        row_sum = sb("row_sum", [P, NT])
        r_inv = sb("r_inv", [P, NT])
        r_w3 = sb("r_w3", [P, NT])
        deg = sb("deg", [P, NT])
        dinv = sb("dinv", [P, NT])
        dinv_eye = work[:, 1, 0:N].rearrange("p (t n) -> p t n", n=P)
        dinv_row = sb("dinv_row", [P, N])
        norm = sb("norm", [P, 6, NT, NG])
        tiny = sb("tiny", [P, 1])
        ps = [ctx.enter_context(nc.psum_tensor(f"bank{i}", [P, 512], F32)) for i in range(8)]

        ps_count = [ps[0], ps[1]]
        ps_h0t = [ps[2], ps[3]]
        ps_bias1 = ps[6][:, 0:HT]
        ps_q = [ps[4], ps[5]]
        ps_tr = [ps[6], ps[7]]
        ps_kp = [ps[2], ps[3]]
        ps_b = [ps[0], ps[1]]
        ps_deg = [ps[2][:, 384:386], ps[3][:, 384:386]]
        ps_dinv = ps[2][:, 0:N]
        ps_bq = [ps[6], ps[7]]
        ps_agg = [ps[0], ps[1], ps[2], ps[3]]
        ps_z = [ps[6], ps[7], ps[0]]
        ps_v = [ps[4], ps[5]]
        ps_out = [ps[2], ps[3]]
        ident = eye[:, 0, 0:P]

        edges_in, dw_in, bias0_in, bias1_in, bias2_in = (
            sem(n) for n in ("edges_in", "dw_in", "bias0_in", "bias1_in", "bias2_in"))
        x_in = [sem(f"x_in{t}") for t in range(NT)]
        unit_in = [sem(f"unit_in{u}") for u in range(UNITS)]
        stored = sem("stored")
        iota_done, consts_done, rstd_done, dinv_done, m_t_done, bias0_lo_done = (
            sem(n) for n in ("iota_done", "consts_done", "rstd_done", "dinv_done", "m_t_done", "bias0_lo_done"))
        hi_done = [sem(f"hi_done{u}") for u in range(UNITS)]
        lo_done = [sem(f"lo_done{u}") for u in range(UNITS)]
        table_ready = sem("table_ready")
        h0_done, bias0_hi_done, bias1_done, h0t_hi_done, count_t_done, wi_hi_done = (
            sem(n) for n in ("h0_done", "bias0_hi_done", "bias1_done", "h0t_hi_done", "count_t_done", "wi_hi_done"))
        poly_hi_done, b_hi_done, q_hi_done, relu_done, dinv_row_done = (
            sem(n) for n in ("poly_hi_done", "b_hi_done", "q_hi_done", "relu_done", "dinv_row_done"))
        root2_done, h1_hi_done, agg_hi_done, z_done, v_hi_done, square_done, root3_done = (
            sem(n) for n in ("root2_done", "h1_hi_done", "agg_hi_done", "z_done", "v_hi_done", "square_done",
                             "root3_done"))
        eye_done, var_done, shift_done, onehot_done, h0t_lo_done, s_done, r_done = (
            sem(n) for n in ("eye_done", "var_done", "shift_done", "onehot_done", "h0t_lo_done", "s_done", "r_done"))
        wi_lo_done, poly_lo_done, b_lo_done, q_lo_done, deg_done, dinv_eye_done = (
            sem(n) for n in ("wi_lo_done", "poly_lo_done", "b_lo_done", "q_lo_done", "deg_done", "dinv_eye_done"))
        x1_done, var2_done, shift2_done, h1_lo_done, agg_done, diag_r_done = (
            sem(n) for n in ("x1_done", "var2_done", "shift2_done", "h1_lo_done", "agg_done", "diag_r_done"))
        z_hi_done, z_lo_done, v_lo_done, v_done, sum_done, out_done, dve_own = (
            sem(n) for n in ("z_hi_done", "z_lo_done", "v_lo_done", "v_done", "sum_done", "out_done", "dve_own"))
        agg_lo_done = [sem(f"agg_lo_done{c}") for c in range(DT)]
        counted, h0t_ps_done, bias1_ps_done, tr_ps_done, kp_ps_done, b_ps_done, q_ps_done = (
            sem(n) for n in ("counted", "h0t_ps_done", "bias1_ps_done", "tr_ps_done", "kp_ps_done", "b_ps_done",
                             "q_ps_done"))
        deg_ps_done, dinv_ps_done, bq_ps_done, agg_ps_done, z_ps_done, z_used, v_ps_done, out_ps_done = (
            sem(n) for n in ("deg_ps_done", "dinv_ps_done", "bq_ps_done", "agg_ps_done", "z_ps_done", "z_used",
                             "v_ps_done", "out_ps_done"))

        w_rows = w.rearrange("(c p) n -> p c n", p=P)
        w1_rows = w1.rearrange("(c p) (u n) -> u p c n", p=P, n=D)
        w2_rows = w2.rearrange("(u c p) n -> u p c n", p=P, c=DT)
        x_rows = x.rearrange("(t p) d -> t p d", p=P)
        out_rows = out.rearrange("(t p) d -> t p d", p=P)

        def unit_dram(u):
            return w_rows if u == 0 else w1_rows[u - 1] if u <= UPM else w2_rows[u - 1 - UPM]

        def w_part(part, c):
            return part[:, slot[0], c, :]

        def w1_part(part, c, j):
            return part[:, slot[1 + j // PER], c, (j % PER) * P:(j % PER + 1) * P]

        def w2_part(part, j):
            return part[:, slot[1 + UPM + j // PER], j % PER, :]

        def work_feat(c):
            return work[:].rearrange("p t d -> p (t d)")[:, c * N:(c + 1) * N]

        def agg_lo(eng, unit, c):
            eng.wait_ge(agg_hi_done, c + 1)
            unit.tensor_tensor(feat_lo[:, c, :], work_feat(c), feat_hi[:, c, :].bitcast(F32),
                               ALU.subtract).then_inc(agg_lo_done[c], 1)

        def split_waits(eng, u, part_done):
            if u == UNITS - 2:
                eng.wait_ge(q_ps_done, NT)
            if u == UNITS - 1:
                eng.wait_ge(z_ps_done, PER)

        block = ctx.enter_context(nc.Block())

        @block.sync
        def _(sp):
            sp.dma_start(edge_i[:, 0, :], src.rearrange("(p t) -> p t", t=ET)).then_inc(edges_in, 16)
            for t in range(NT):
                sp.dma_start(x_sb[:, t, :], x_rows[t]).then_inc(x_in[t], 16)
            for u in range(UNITS):
                if u >= RAW:
                    sp.wait_ge(hi_done[u - RAW], DT)
                    sp.wait_ge(lo_done[u - RAW], DT)
                sp.dma_start(raw[:, u % RAW], unit_dram(u)).then_inc(unit_in[u], 16)
            for t in range(NT):
                sp.wait_ge(out_done, t + 1)
                sp.dma_start(out_rows[t], work[:, t, :]).then_inc(stored, 16)
            sp.wait_ge(stored, 16 * NT)

        @block.gpsimd
        def _(pool):
            nc.gpsimd.iota(column[:], [[1, N], [0, 2]], base=0, channel_multiplier=0,
                           allow_small_or_imprecise_dtypes=True).then_inc(iota_done, 1)
            nc.gpsimd.iota(row[:], [[P, NT]], base=0, channel_multiplier=1,
                           allow_small_or_imprecise_dtypes=True).then_inc(iota_done, 1)
            nc.gpsimd.memset(minus_half[:], -0.5).then_inc(consts_done, 1)
            nc.gpsimd.memset(ones_r[:].bitcast(F32), 1.0).then_inc(consts_done, 1)
            nc.gpsimd.memset(tiny[:], TINY).then_inc(consts_done, 1)
            pool.wait_ge(consts_done, 1)
            pool.wait_ge(var_done, 1)
            nc.gpsimd.tensor_tensor(rstd[:], var_eps[:], minus_half[:], ALU.pow).then_inc(rstd_done, 1)

            def split_lo(u, c):
                pool.wait_ge(hi_done[u], c + 1)
                split_waits(pool, u, lo_done)
                nc.gpsimd.tensor_tensor(wt_lo[:, slot[u], c, :], raw[:, u % RAW, c, :],
                                        wt_hi[:, slot[u], c, :].bitcast(F32), ALU.subtract).then_inc(lo_done[u], 1)

            for c in range(DT):
                split_lo(0, c)
            pool.wait_ge(bias0_hi_done, 1)
            nc.gpsimd.tensor_tensor(bias0_lo, bias0, bias0_hi.bitcast(F32),
                                    ALU.subtract).then_inc(bias0_lo_done, 1)
            for c in range(DT):
                split_lo(1, c)
            pool.wait_ge(eye_done, NT)
            for t in range(NT):
                pool.wait_ge(count_t_done, t + 1)
                nc.gpsimd.tensor_tensor(m_t[:, t, :], count_t[:, t, :], eye[:, t, :], ALU.add).then_inc(m_t_done, 1)
            pool.wait_ge(deg_done, NT)
            nc.gpsimd.tensor_tensor(dinv[:], deg[:], minus_half[:], ALU.pow).then_inc(dinv_done, 1)
            for c in range(DT):
                split_lo(3, c)
            for c in range(2):
                split_lo(4, c)
            for c in range(DT // 2):
                agg_lo(pool, nc.gpsimd, c)
            for c in range(DT):
                split_lo(5, c)
            for c in range(2, DT):
                split_lo(4, c)
            for u in range(6, UNITS):
                for c in range(DT):
                    split_lo(u, c)

        @block.scalar
        def _(act):
            act.dma_start(edge_i[:, 1, :], dst.rearrange("(p t) -> p t", t=ET)).then_inc(edges_in, 16)
            act.dma_start(dw_sb[:], dw.partition_broadcast(P)).then_inc(dw_in, 16)
            act.dma_start(bias0, b.rearrange("(o k) -> o k", o=1)).then_inc(bias0_in, 16)
            act.dma_start(bias1_rows[:], b1.rearrange("(j p) -> j p", p=P)).then_inc(bias1_in, 16)
            act.dma_start(bias2[:], b2.partition_broadcast(P)).then_inc(bias2_in, 16)

            def split_hi(u, c):
                if c == 0:
                    act.wait_ge(unit_in[u], 16)
                    split_waits(act, u, hi_done)
                nc.scalar.activation(wt_hi[:, slot[u], c, :], raw[:, u % RAW, c, :], ACT.Copy).then_inc(hi_done[u], 1)

            act.wait_ge(consts_done, 2)
            nc.scalar.activation(ready[:], ones_r[:, 0:1].bitcast(F32), ACT.Sqrt).then_inc(table_ready, 1)
            for c in range(DT):
                split_hi(0, c)
            act.wait_ge(shift_done, 1)
            for t in range(NT):
                nc.scalar.activation(work[:, t, :], x_sb[:, t, :], ACT.Relu, bias=shift[:, t:t + 1],
                                     scale=rstd[:, t:t + 1]).then_inc(h0_done, 1)
            act.wait_ge(bias0_in, 16)
            nc.scalar.activation(bias0_hi, bias0, ACT.Copy).then_inc(bias0_hi_done, 1)
            for t in range(2):
                act.wait_ge(h0t_ps_done, t + 1)
                nc.scalar.activation(feat_hi[:, 2 * t:2 * t + 2, :], ps_h0t[t][:].rearrange("p (c n) -> p c n", n=N),
                                     ACT.Copy).then_inc(h0t_hi_done, 1)
            act.wait_ge(dw_in, 16)
            act.wait_ge(eye_done, NT)
            for k in range(3):
                nc.scalar.activation(wi_hi[:, k, :], ident, ACT.Copy, scale=dw_sb[:, k:k + 1]).then_inc(wi_hi_done, 1)
            for c in range(DT):
                split_hi(1, c)
            for c in range(2):
                split_hi(2, c)
            act.wait_ge(bias1_ps_done, 1)
            nc.scalar.activation(bias1[:], ps_bias1, ACT.Copy).then_inc(bias1_done, 1)
            for t in range(NT):
                act.wait_ge(counted, PAIRS)
                nc.scalar.activation(count_t[:, t, :], ps_count[t][:, 0:N], ACT.Copy).then_inc(count_t_done, 1)

            def q_hi(t):
                act.wait_ge(q_ps_done, t + 1)
                nc.scalar.activation(node_hi[:, t, :], ps_q[t][:], ACT.Copy).then_inc(q_hi_done, 1)

            q_hi(0)
            for t in range(NT):
                act.wait_ge(r_done, 1)
                nc.scalar.activation(poly_hi[:, t, :], s_adj[:, t, :].bitcast(F32), ACT.Copy,
                                     scale=r_w3[:, t:t + 1]).then_inc(poly_hi_done, 1)
            split_hi(2, 2)
            for t in range(NT):
                act.wait_ge(kp_ps_done, t + 1)
                nc.scalar.activation(poly_hi[:, t, :], ps_kp[t][:, 0:N], ACT.Copy,
                                     scale=r_inv[:, t:t + 1]).then_inc(poly_hi_done, 1)
            split_hi(2, 3)
            for t in range(NT):
                act.wait_ge(b_ps_done, t + 1)
                nc.scalar.activation(b_hi[:, t, :], ps_b[t][:, 0:N], ACT.Copy).then_inc(b_hi_done, 1)
            q_hi(1)
            for c in range(2):
                split_hi(3, c)
            for t in range(NT):
                act.wait_ge(bq_ps_done, t + 1)
                nc.scalar.activation(temp[:, t, :], ps_bq[t][:], ACT.Relu, scale=r_inv[:, t:t + 1]).then_inc(relu_done, 1)
            act.wait_ge(dinv_ps_done, 1)
            nc.scalar.activation(dinv_row[:], ps_dinv, ACT.Copy).then_inc(dinv_row_done, 1)
            split_hi(3, 2)
            for t in range(NT):
                act.wait_ge(var2_done, t + 1)
                nc.scalar.activation(root2[:, t:t + 1], var_eps2[:, t:t + 1], ACT.Sqrt).then_inc(root2_done, 1)
                if t == 0:
                    split_hi(3, 3)
            split_hi(4, 0)
            for t in range(NT):
                act.wait_ge(shift2_done, t + 1)
                for k in range(2):
                    at = slice(k * HALF, (k + 1) * HALF)
                    nc.scalar.activation(node_hi[:, t, at], x_sb[:, t, at], ACT.Relu, bias=shift2[:, t:t + 1],
                                         scale=scale2[:, t:t + 1]).then_inc(h1_hi_done, 1)
            split_hi(4, 1)
            for c in range(DT):
                act.wait_ge(agg_done, c + 1)
                nc.scalar.activation(feat_hi[:, c, :], work_feat(c), ACT.Copy).then_inc(agg_hi_done, 1)
            for c in range(2):
                split_hi(5, c)
            for j in range(HT):
                act.wait_ge(z_ps_done, j + 1)
                if j >= ZR:
                    act.wait_ge(z_lo_done, j - ZR + 1)
                if j == 0:
                    act.wait_ge(bias1_done, 1)
                nc.scalar.activation(z_sb[:, j % ZR, :], ps_z[j % ZR][:, 0:N], ACT.Relu,
                                     bias=bias1[:, j:j + 1]).then_inc(z_done, 1)
                if j == 0:
                    for c in range(2, DT):
                        split_hi(5, c)
                if j == 1:
                    for c in range(2, DT):
                        split_hi(4, c)
                u = 6 + (j - 3) // 2
                if j >= 3 and u < UNITS:
                    for c in range(DT // 2):
                        split_hi(u, (j - 3) % 2 * (DT // 2) + c)
            for t in range(NT):
                act.wait_ge(v_ps_done, t + 1)
                nc.scalar.activation(node_hi[:, t, :], ps_v[t][:], ACT.Copy, scale=dinv[:, t:t + 1]).then_inc(v_hi_done, 1)
            for t in range(NT):
                act.wait_ge(v_done, t + 1)
                nc.scalar.activation(temp[:, t, :], work[:, t, :], ACT.Square).then_inc(square_done, 1)
            act.wait_ge(sum_done, NT)
            nc.scalar.activation(norm[:, 1], norm[:, 0], ACT.Sqrt, bias=tiny[:]).then_inc(root3_done, 1)

        @block.vector
        def _(dve):
            own = [0]

            def mine(ins):
                own[0] += 1
                ins.then_inc(dve_own, 1)
                return own[0]

            def after(ins):
                dve.wait_ge(dve_own, mine(ins))

            def split_lo(u, c):
                dve.wait_ge(hi_done[u], c + 1)
                nc.vector.tensor_tensor(wt_lo[:, slot[u], c, :], raw[:, u % RAW, c, :],
                                        wt_hi[:, slot[u], c, :].bitcast(F32), ALU.subtract).then_inc(lo_done[u], 1)

            dve.wait_ge(iota_done, 2)
            for t in range(NT):
                nc.vector.tensor_scalar(eye[:, t, :], column[:, :, 0], row[:, t:t + 1], None, ALU.is_equal).then_inc(eye_done, 1)
            dve.wait_ge(edges_in, 32)
            after(nc.vector.tensor_copy(edge_b[:], edge_i[:]))

            def onehot(q):
                if q >= ONEHOTS:
                    dve.wait_ge(counted, q - ONEHOTS + 1)
                full = [P, 2, N, 2]
                nc.vector.tensor_tensor(onehots[:, q % ONEHOTS],
                                        edge_b[:, :, 2 * q:2 * q + 2].unsqueeze(2).broadcast_to(full),
                                        column[:].unsqueeze(1).broadcast_to(full), ALU.is_equal).then_inc(onehot_done, 1)

            onehot(0)
            onehot(1)
            for t in range(NT):
                dve.wait_ge(x_in[t], 16)
                n_stats = mine(nc.vector.bn_stats(stats[:, t, :], x_sb[:, t, :]))
                onehot(2 + t)
            dve.wait_ge(dve_own, n_stats)
            for t in range(NT):
                n_aggr = mine(nc.vector.bn_aggr(mean_var[:, t, :], stats[:, t, :]))
            onehot(4)
            dve.wait_ge(dve_own, n_aggr)
            nc.vector.tensor_scalar(var_eps[:], mean_var[:, :, 1], EPS, None, ALU.add).then_inc(var_done, 1)
            onehot(5)
            dve.wait_ge(rstd_done, 1)
            nc.vector.scalar_tensor_tensor(out=shift[:], in0=mean_var[:, :, 0], scalar=-1.0, in1=rstd[:],
                                           op0=ALU.mult, op1=ALU.mult).then_inc(shift_done, 1)
            for q in range(6, 11):
                onehot(q)
            for k in range(2):
                dve.wait_ge(h0t_hi_done, k + 1)
                nc.vector.tensor_tensor(feat_lo[:, 2 * k:2 * k + 2, :], ps_h0t[k][:].rearrange("p (c n) -> p c n", n=N),
                                        feat_hi[:, 2 * k:2 * k + 2, :].bitcast(F32), ALU.subtract).then_inc(h0t_lo_done, 1)
                onehot(11 + k)
            for q in range(13, PAIRS):
                onehot(q)
            for k in range(3):
                dve.wait_ge(wi_hi_done, k + 1)
                nc.vector.scalar_tensor_tensor(out=wi_lo[:, k, :], in0=ident, scalar=dw_sb[:, k:k + 1],
                                               in1=wi_hi[:, k, :].bitcast(F32), op0=ALU.mult,
                                               op1=ALU.subtract).then_inc(wi_lo_done, 1)
            for t in range(NT):
                dve.wait_ge(tr_ps_done, t + 1)
                dve.wait_ge(count_t_done, t + 1)
                after(nc.vector.tensor_tensor(both[:, t, :], ps_tr[t][:, 0:N], count_t[:, t, :], ALU.add))
                nc.vector.scalar_tensor_tensor(out=s_adj[:, t, :], in0=both[:, t, :], scalar=1.0,
                                               in1=eye[:, t, :], op0=ALU.min, op1=ALU.add,
                                               accum_out=row_sum[:, t:t + 1]).then_inc(s_done, 1)
            dve.wait_ge(s_done, NT)
            after(nc.vector.reciprocal(r_inv[:], row_sum[:]))
            nc.vector.tensor_scalar(r_w3[:], r_inv[:], dw_sb[:, 3:4], None, ALU.mult).then_inc(r_done, 1)
            for t in range(NT):
                nc.vector.tensor_scalar(diag_r[:, t, :], ident, row_sum[:, t:t + 1], None, ALU.mult).then_inc(diag_r_done, 1)
            for t in range(NT):
                dve.wait_ge(poly_hi_done, t + 1)
                dve.wait_ge(r_done, 1)
                nc.vector.scalar_tensor_tensor(out=poly_lo[:, t, :], in0=s_adj[:, t, :].bitcast(F32),
                                               scalar=r_w3[:, t:t + 1], in1=poly_hi[:, t, :].bitcast(F32),
                                               op0=ALU.mult, op1=ALU.subtract).then_inc(poly_lo_done, 1)

            def q_lo(t):
                dve.wait_ge(q_hi_done, t + 1)
                nc.vector.tensor_tensor(node_lo[:, t, :], ps_q[t][:], node_hi[:, t, :].bitcast(F32),
                                        ALU.subtract).then_inc(q_lo_done, 1)

            q_lo(0)
            for t in range(NT):
                dve.wait_ge(poly_hi_done, NT + t + 1)
                nc.vector.scalar_tensor_tensor(out=poly_lo[:, t, :], in0=ps_kp[t][:, 0:N], scalar=r_inv[:, t:t + 1],
                                               in1=poly_hi[:, t, :].bitcast(F32), op0=ALU.mult,
                                               op1=ALU.subtract).then_inc(poly_lo_done, 1)
            split_lo(2, 0)
            for t in range(NT):
                dve.wait_ge(b_hi_done, t + 1)
                nc.vector.tensor_tensor(b_lo[:, t, :], ps_b[t][:, 0:N], b_hi[:, t, :].bitcast(F32),
                                        ALU.subtract).then_inc(b_lo_done, 1)
            q_lo(1)
            for t in range(NT):
                dve.wait_ge(deg_ps_done, t + 1)
                nc.vector.tensor_copy(deg[:, t:t + 1], ps_deg[t][:, 0:1]).then_inc(deg_done, 1)
            for c in range(1, DT):
                split_lo(2, c)
            for t in range(NT):
                dve.wait_ge(dinv_done, 1)
                nc.vector.tensor_scalar(dinv_eye[:, t, :], ident, dinv[:, t:t + 1], None, ALU.mult).then_inc(dinv_eye_done, 1)

            def x1(t):
                dve.wait_ge(relu_done, t + 1)
                nc.vector.tensor_tensor(x_sb[:, t, :], temp[:, t, :], x_sb[:, t, :], ALU.add).then_inc(x1_done, 1)

            def x1_stats(t):
                dve.wait_ge(x1_done, t + 1)
                return mine(nc.vector.bn_stats(stats2[:, t, :], x_sb[:, t, :]))

            def x1_moments(t, n_stats):
                dve.wait_ge(dve_own, n_stats)
                after(nc.vector.bn_aggr(mean_var2[:, t, :], stats2[:, t, :]))
                nc.vector.tensor_scalar(var_eps2[:, t:t + 1], mean_var2[:, t, 1:2], EPS, None, ALU.add).then_inc(var2_done, 1)

            def x1_scale(t):
                at = slice(t, t + 1)
                dve.wait_ge(root2_done, t + 1)
                after(nc.vector.reciprocal(inv2[:, at], root2[:, at]))
                dve.wait_ge(var2_done, t + 1)
                n_a = mine(nc.vector.tensor_tensor(newton_a[:, at], var_eps2[:, at], inv2[:, at], ALU.mult))
                n_d = mine(nc.vector.tensor_tensor(inv2_dinv[:, at], inv2[:, at], dinv[:, at], ALU.mult))
                dve.wait_ge(dve_own, n_a)
                n_b = mine(nc.vector.scalar_tensor_tensor(out=newton_b[:, at], in0=newton_a[:, at], scalar=-0.5,
                                                          in1=inv2[:, at], op0=ALU.mult, op1=ALU.mult))
                dve.wait_ge(dve_own, max(n_b, n_d))
                after(nc.vector.scalar_tensor_tensor(out=scale2[:, at], in0=newton_b[:, at], scalar=1.5,
                                                     in1=inv2_dinv[:, at], op0=ALU.add, op1=ALU.mult))
                nc.vector.scalar_tensor_tensor(out=shift2[:, at], in0=mean_var2[:, t, 0:1], scalar=-1.0,
                                               in1=scale2[:, at], op0=ALU.mult, op1=ALU.mult).then_inc(shift2_done, 1)

            def x1_norm(t):
                dve.wait_ge(shift2_done, t + 1)
                return mine(nc.vector.tensor_scalar(temp[:, t, :], x_sb[:, t, :], scale2[:, t:t + 1],
                                                    shift2[:, t:t + 1], ALU.mult, ALU.add))

            def h1_lo(t, n_norm):
                dve.wait_ge(dve_own, n_norm)
                for k in range(2):
                    at = slice(k * HALF, (k + 1) * HALF)
                    dve.wait_ge(h1_hi_done, 2 * t + k + 1)
                    nc.vector.scalar_tensor_tensor(out=node_lo[:, t, at], in0=temp[:, t, at], scalar=0.0,
                                                   in1=node_hi[:, t, at].bitcast(F32), op0=ALU.max,
                                                   op1=ALU.subtract).then_inc(h1_lo_done, 1)

            x1(0)
            n_stats = x1_stats(0)
            x1_moments(0, n_stats)
            x1(1)
            n_stats = x1_stats(1)
            x1_moments(1, n_stats)
            x1_scale(0)
            n_norm0 = x1_norm(0)
            x1_scale(1)
            h1_lo(0, n_norm0)
            n_norm1 = x1_norm(1)
            h1_lo(1, n_norm1)

            dve.wait_ge(dinv_row_done, 1)
            for c in range(DT):
                dve.wait_ge(agg_ps_done, c + 1)
                nc.vector.tensor_tensor(work_feat(c), ps_agg[c][:, 0:N], dinv_row[:], ALU.mult).then_inc(agg_done, 1)
            for c in range(DT // 2, DT):
                agg_lo(dve, nc.vector, c)
            for j in range(HT):
                dve.wait_ge(z_done, j + 1)
                if j >= ZR:
                    dve.wait_ge(z_used, j - ZR + 1)
                nc.vector.tensor_copy(z_hi[:, j % ZR, :], z_sb[:, j % ZR, :]).then_inc(z_hi_done, 1)
                dve.wait_ge(z_hi_done, j + 1)
                nc.vector.tensor_tensor(z_lo[:, j % ZR, :], z_sb[:, j % ZR, :], z_hi[:, j % ZR, :].bitcast(F32),
                                        ALU.subtract).then_inc(z_lo_done, 1)
            for t in range(NT):
                dve.wait_ge(v_hi_done, t + 1)
                nc.vector.scalar_tensor_tensor(out=node_lo[:, t, :], in0=ps_v[t][:], scalar=dinv[:, t:t + 1],
                                               in1=node_hi[:, t, :].bitcast(F32), op0=ALU.mult,
                                               op1=ALU.subtract).then_inc(v_lo_done, 1)
            dve.wait_ge(bias2_in, 16)
            for t in range(NT):
                dve.wait_ge(out_ps_done, t + 1)
                nc.vector.scalar_tensor_tensor(out=work[:, t, :], in0=ps_out[t][:], scalar=dinv[:, t:t + 1],
                                               in1=bias2[:], op0=ALU.mult, op1=ALU.add).then_inc(v_done, 1)
            for t in range(NT):
                dve.wait_ge(square_done, t + 1)
                nc.vector.tensor_reduce(norm[:, 0, t, :], temp[:, t, :].rearrange("p (g k) -> p g k", k=GROUP),
                                        AX.X, ALU.add).then_inc(sum_done, 1)
            total, root, inv, step_a, step_b, scale = (norm[:, k] for k in range(6))
            dve.wait_ge(root3_done, 1)
            after(nc.vector.reciprocal(inv, root))
            dve.wait_ge(sum_done, NT)
            after(nc.vector.scalar_tensor_tensor(out=step_a, in0=total, scalar=-0.5, in1=inv, op0=ALU.mult, op1=ALU.mult))
            after(nc.vector.tensor_tensor(step_b, step_a, inv, ALU.mult))
            after(nc.vector.scalar_tensor_tensor(out=scale, in0=step_b, scalar=1.5, in1=inv, op0=ALU.add, op1=ALU.mult))
            for t in range(NT):
                after(nc.vector.scalar_tensor_tensor(
                    out=temp[:, t, :].rearrange("p (g k) -> p g k", k=GROUP),
                    in0=scale[:, t, :].unsqueeze(2).broadcast_to([P, NG, GROUP]), scalar=1.0 / NORM_FLOOR,
                    in1=work[:, t, :].rearrange("p (g k) -> p g k", k=GROUP), op0=ALU.min, op1=ALU.mult))
                nc.vector.tensor_tensor(work[:, t, :], temp[:, t, :], x_sb[:, t, :], ALU.add).then_inc(out_done, 1)

        @block.tensor
        def _(pe):
            def product(bank, terms, done=None, start=True, stop=True):
                for i, (stationary, moving) in enumerate(terms):
                    last = nc.tensor.matmul(bank, stationary, moving, start=start and i == 0,
                                            stop=stop and i == len(terms) - 1)
                if done is not None:
                    last.then_inc(done, 1)

            def q_terms(t):
                at = slice(t * P, (t + 1) * P)
                high = [(part[:, c, at], w_part(wt_hi, c)) for part in (feat_hi, feat_lo) for c in range(DT)]
                low = [(feat_hi[:, c, at], w_part(wt_lo, c)) for c in range(DT)]
                return high + [(ones_r[0:1, :], bias0_hi), (ones_r[0:1, :], bias0_lo)], low

            high0, low0 = q_terms(0)
            high1, low1 = q_terms(1)
            for q in range(PAIRS):
                pe.wait_ge(onehot_done, q + 1)
                for e in range(2):
                    for s in range(NT):
                        last = nc.tensor.matmul(ps_count[s][:, 0:N], onehots[:, q % ONEHOTS, 0, s * P:(s + 1) * P, e],
                                                onehots[:, q % ONEHOTS, 1, :, e], start=q + e == 0,
                                                stop=q == PAIRS - 1 and e == 1)
                last.then_inc(counted, 1)
                if q == 6:
                    pe.wait_ge(eye_done, NT)
                    pe.wait_ge(bias1_in, 16)
                    nc.tensor.transpose(ps_bias1, bias1_rows[:], ident[0:HT, 0:HT]).then_inc(bias1_ps_done, 1)
                if q == 8:
                    pe.wait_ge(h0_done, NT)
                    for k in range(2):
                        for c in (2 * k, 2 * k + 1):
                            for n in range(NT):
                                at = (c % 2) * N + n * P
                                last = nc.tensor.transpose(ps_h0t[k][:, at:at + P], work[:, n, c * P:(c + 1) * P], ident)
                        last.then_inc(h0t_ps_done, 1)
                if q == 13:
                    pe.wait_ge(h0t_hi_done, 2)
                    pe.wait_ge(hi_done[0], DT)
                    product(ps_q[0][:], high0[:4], stop=False)
                if q == 14:
                    pe.wait_ge(h0t_lo_done, 2)
                    product(ps_q[0][:], high0[4:8], start=False, stop=False)
                if q == 15:
                    pe.wait_ge(consts_done, 2)
                    pe.wait_ge(bias0_lo_done, 1)
                    product(ps_q[0][:], high0[8:], start=False, stop=False)
            pe.wait_ge(bias1_done, 1)
            for t in range(NT):
                pe.wait_ge(count_t_done, NT)
                for s in range(NT):
                    last = nc.tensor.transpose(ps_tr[t][:, s * P:(s + 1) * P], count_t[:, s, t * P:(t + 1) * P], ident)
                last.then_inc(tr_ps_done, 1)

            pe.wait_ge(lo_done[0], DT)
            product(ps_q[0][:], low0, q_ps_done, start=False)
            product(ps_q[1][:], high1[:5], stop=False)

            def times_s(banks, k, before, poly_count, done):
                for m in range(NT):
                    at = slice(m * P, (m + 1) * P)
                    first = before(m)
                    for c in range(NT):
                        for part in (wi_hi, wi_lo):
                            nc.tensor.matmul(banks[m][:, c * P:(c + 1) * P], s_adj[:, c, at], part[:, k, :],
                                             start=first, stop=False, skip_group_check=True)
                            first = False
                for c in range(NT):
                    pe.wait_ge(poly_lo_done, poly_count + c + 1)
                    for m in range(NT):
                        at = slice(m * P, (m + 1) * P)
                        for part in (poly_hi, poly_lo):
                            last = nc.tensor.matmul(banks[m][:, 0:N], s_adj[:, c, at], part[:, c, :], start=False,
                                                    stop=c == NT - 1 and part is poly_lo, skip_group_check=True)
                        if c == NT - 1:
                            last.then_inc(done, 1)

            def add_w0_r(m):
                for i, part in enumerate((wi_hi, wi_lo)):
                    nc.tensor.matmul(ps_b[m][:, m * P:(m + 1) * P], diag_r[:, m, :], part[:, 0, :], start=i == 0,
                                     stop=False, skip_group_check=True)
                return False

            pe.wait_ge(s_done, NT)
            pe.wait_ge(wi_lo_done, 3)
            times_s(ps_kp, 2, lambda m: True, 0, kp_ps_done)
            product(ps_q[1][:], high1[5:], start=False, stop=False)
            pe.wait_ge(diag_r_done, NT)
            times_s(ps_b, 1, add_w0_r, NT, b_ps_done)
            product(ps_q[1][:], low1, q_ps_done, start=False)
            pe.wait_ge(m_t_done, NT)
            for t in range(NT):
                product(ps_deg[t], [(m_t[:, s, t * P:(t + 1) * P], ones_r[:, 0:2]) for s in range(NT)], deg_ps_done)
            pe.wait_ge(b_lo_done, NT)
            pe.wait_ge(q_lo_done, NT)
            for t in range(NT):
                at = slice(t * P, (t + 1) * P)
                product(ps_bq[t][:], [(l[:, s, at], r[:, s, :]) for s in range(NT)
                                      for l, r in ((b_hi, node_hi), (b_lo, node_hi), (b_hi, node_lo))], bq_ps_done)
            pe.wait_ge(dinv_eye_done, NT)
            for t in range(NT):
                last = nc.tensor.matmul(ps_dinv[:, t * P:(t + 1) * P], ones_r[:].bitcast(F32), dinv_eye[:, t, :],
                                        start=True, stop=True)
            last.then_inc(dinv_ps_done, 1)
            pe.wait_ge(dinv_row_done, 1)
            for s in range(NT):
                for c in range(DT):
                    pe.wait_ge(h1_lo_done, 2 * s + c * P // HALF + 1)
                    product(ps_agg[c][:, 0:N], [(part[:, s, c * P:(c + 1) * P], m_t[:, s, :])
                                                for part in (node_hi, node_lo)],
                            agg_ps_done if s == NT - 1 else None, start=s == 0, stop=s == NT - 1)

            def hidden(j):
                pe.wait_ge(lo_done[1 + j // PER], DT)
                if j >= ZR:
                    pe.wait_ge(z_done, j - ZR + 1)
                for c in range(DT):
                    if j == 0:
                        pe.wait_ge(agg_lo_done[c], 1)
                    product(ps_z[j % ZR][:, 0:N], [(w1_part(l, c, j), r[:, c, :]) for l, r in
                                                   ((wt_hi, feat_hi), (wt_hi, feat_lo), (wt_lo, feat_hi))],
                            z_ps_done if c == DT - 1 else None, start=c == 0, stop=c == DT - 1)

            def project(j, t, done=None):
                pe.wait_ge(z_lo_done, j + 1)
                pe.wait_ge(lo_done[1 + UPM + j // PER], j % PER + 1)
                at = slice(t * P, (t + 1) * P)
                product(ps_v[t][:], [(l[:, j % ZR, at], w2_part(r, j))
                                     for l, r in ((z_hi, wt_hi), (z_lo, wt_hi), (z_hi, wt_lo))],
                        done, start=j == 0, stop=j == HT - 1)

            LAG = 2
            for j in range(HT):
                hidden(j)
                if j >= LAG:
                    project(j - LAG, 0)
                    project(j - LAG, 1, z_used)
            for t in range(NT):
                for j in range(HT - LAG, HT):
                    project(j, t, v_ps_done if j == HT - 1 else None)
            for s in range(NT):
                pe.wait_ge(v_lo_done, s + 1)
                for t in range(NT):
                    at = slice(t * P, (t + 1) * P)
                    product(ps_out[t][:], [(m_t[:, s, at], part[:, s, :]) for part in (node_hi, node_lo)],
                            out_ps_done if s == NT - 1 else None, start=s == 0, stop=s == NT - 1)


_INS = ['x', 'src', 'dst', 'L0_gnn_W', 'L0_gnn_b', 'L0_gnn_diffusion_weights', 'L1_gnn_W1', 'L1_gnn_b1', 'L1_gnn_W2',
        'L1_gnn_b2']


def kernel(**inputs):
    import numpy as _np
    import concourse.bacc as _bacc
    from concourse import mybir as _mybir
    from concourse.bass_utils import run_bass_kernel_spmd as _run

    nc = _bacc.Bacc("TRN2", target_bir_lowering=False, num_devices=1)
    arrays, args = {}, []
    for name in _INS:
        a = _np.ascontiguousarray(inputs[name])
        arrays[f"in_{name}"] = a
        args.append(nc.dram_tensor(f"in_{name}", a.shape, _mybir.dt.from_np(a.dtype), kind="ExternalInput").ap())
    out = nc.dram_tensor("out", inputs['x'].shape, _mybir.dt.float32, kind="ExternalOutput").ap()
    gnn_block(nc, *args, out)
    r = _run(nc, [arrays], core_ids=[0])
    return r.results[0]["out"]
```

```python
from contextlib import ExitStack

import concourse.bass as bass
from concourse import mybir

F32 = mybir.dt.float32
F32R = mybir.dt.float32r
BF16 = mybir.dt.bfloat16
I32 = mybir.dt.int32
ALU = mybir.AluOpType
ACT = mybir.ActivationFunctionType
AX = mybir.AxisListType

P = 128
EPS = 1e-5
NORM_FLOOR = 1e-12
GROUP = 64
TINY = 1e-30


def gnn_block(nc, x, src, dst, w, b, dw, w1, b1, w2, b2, out):
    N, D = x.shape
    E = src.shape[0]
    H = w1.shape[1]
    NT = N // P
    DT = D // P
    HT = H // P
    ET = E // P
    NG = D // GROUP
    UPM = H // D
    PER = D // P
    PAIRS = ET // 2
    assert ET % 2 == 0 and NT == 2
    ONEHOTS = 6
    GROUPS = [2] * ((PAIRS - 3) // 2) + [1] * (PAIRS - (PAIRS - 3) // 2 * 2)
    HALF = D // 2
    ZR = 3
    AGG_ORDER = *range(1, DT), 0
    WARM_START = 18
    WARM_NORM = 8, 6

    UNITS = 1 + 2 * UPM
    RAW = 3
    SLOTS = UNITS - 2
    slot = [u if u < SLOTS else u - SLOTS for u in range(UNITS)]

    with ExitStack() as ctx:
        def sb(name, shape, dt=F32):
            return ctx.enter_context(nc.sbuf_tensor(name, shape, dt))

        def sem(name):
            return ctx.enter_context(nc.semaphore(name))

        raw = sb("raw", [P, RAW, DT, D])
        wt_hi = sb("wt_hi", [P, SLOTS, DT, D], F32R)
        wt_lo = sb("wt_lo", [P, SLOTS, DT, D], F32R)
        x_sb = sb("x_sb", [P, NT, D])
        work = sb("work", [P, NT, D])
        temp = sb("temp", [P, NT, D])
        feat_hi = sb("feat_hi", [P, DT, N], F32R)
        feat_lo = sb("feat_lo", [P, DT, N], F32R)
        node_hi = sb("node_hi", [P, NT, D], F32R)
        node_lo = sb("node_lo", [P, NT, D], F32R)
        z_sb = sb("z_sb", [P, ZR, N])
        z_hi = sb("z_hi", [P, ZR, N], F32R)
        z_lo = sb("z_lo", [P, ZR, N], F32R)
        onehots = sb("onehots", [P, ONEHOTS, 2, N, 2], BF16)
        count_b = sb("count_b", [P, NT, N], BF16)
        m_t = sb("m_t", [P, NT, N], F32R)
        s_adj = sb("s_adj", [P, NT, N], F32R)
        poly_hi = sb("poly_hi", [P, NT, N], F32R)
        poly_lo = sb("poly_lo", [P, NT, N], F32R)
        b_sum = temp[:, 1, :].rearrange("p (t n) -> p t n", n=N)
        s_w1 = work[:, 0, :].rearrange("p (t n) -> p t n", n=N)
        b_hi = sb("b_hi", [P, NT, N], F32R)
        b_lo = sb("b_lo", [P, NT, N], F32R)
        column = sb("column", [P, N, 2], BF16)
        row = sb("row", [P, NT])
        ones_r = sb("ones_r", [P, P], F32R)
        eye = sb("eye", [P, NT, N])
        ident_b = sb("ident_b", [P, P], BF16)
        filler = ones_r[:].bitcast(BF16)
        edge_i = sb("edge_i", [P, 2, ET], I32)
        edge_b = sb("edge_b", [P, PAIRS, 2, 2], BF16)
        ready = sb("ready", [P, 1])
        bias0 = temp[0:1, 0, :]
        bias0_hi = b_hi[0:1].rearrange("p t n -> p (t n)")
        bias0_lo = b_lo[0:1].rearrange("p t n -> p (t n)")
        deg_root_parts = s_adj[0:1].rearrange("p t n -> p (t n)")
        bias2 = sb("bias2", [1, D])
        bias2_hi = poly_hi[0:1].rearrange("p t n -> p (t n)")
        bias2_lo = poly_lo[0:1].rearrange("p t n -> p (t n)")
        bias1_rows = sb("bias1_rows", [HT, P])
        bias1 = sb("bias1", [P, HT])
        dw_sb = sb("dw_sb", [P, 4])
        stats = sb("stats", [P, NT, 6])
        mean_var = sb("mean_var", [P, NT, 2])
        var_eps = sb("var_eps", [P, NT])
        minus_half = sb("minus_half", [P, NT])
        rstd = sb("rstd", [P, NT])
        shift = sb("shift", [P, NT])
        stats2 = sb("stats2", [P, NT, 6])
        mean_var2 = sb("mean_var2", [P, NT, 2])
        var_eps2, rstd2, scale2, shift2 = (
            sb(n, [P, NT]) for n in ("var_eps2", "rstd2", "scale2", "shift2"))
        row_sum = sb("row_sum", [P, NT])
        r_inv = sb("r_inv", [P, NT])
        r_hi = sb("r_hi", [P, NT], F32R)
        r_lo = sb("r_lo", [P, NT])
        r_w3 = sb("r_w3", [P, NT])
        r_w0 = sb("r_w0", [P, NT])
        deg = sb("deg", [P, NT])
        dinv = sb("dinv", [P, NT])
        dinv_eye = work[:, 1, 0:N].rearrange("p (t n) -> p t n", n=P)
        dinv_row = sb("dinv_row", [P, N])
        total, root, inv, step_a, step_b, scale, factor = (
            z_sb[:, 0, k * NT * NG:(k + 1) * NT * NG].rearrange("p (h t g) -> p h t g", h=2, t=NT) for k in range(7))
        tiny = sb("tiny", [P, 1])
        floor_scale = sb("floor_scale", [P, NT])
        deg_root = sb("deg_root", [P, NT])
        root_hi = sb("root_hi", [P, NT], F32R)
        root_lo = sb("root_lo", [P, NT])
        ps = [ctx.enter_context(nc.psum_tensor(f"bank{i}", [P, 512], F32)) for i in range(8)]

        ps_count = [ps[0], ps[1]]
        ps_h0t = [ps[2], ps[3]]
        ps_bias1 = ps[6][:, 0:HT]
        ps_q = [ps[4], ps[5]]
        ps_tr = [ps[6], ps[7]]
        ps_srs = [ps[2], ps[3]]
        ps_b = [ps[6], ps[7]]
        ps_deg = [ps[0][:, 0:2], ps[1][:, 0:2]]
        ps_dinv = ps[2][:, 0:N]
        ps_bq = [ps[0], ps[1]]
        ps_agg = [ps[1], ps[0], ps[2], ps[3]]
        ps_z = [ps[6], ps[7], ps[0]]
        V_PARTS = [(0, slice(0, D), ps[2]), (1, slice(0, HALF), ps[3]), (1, slice(HALF, D), ps[1])]
        ps_out = [ps[4], ps[5]]
        halves = [slice(k * HALF, (k + 1) * HALF) for k in range(2)]
        ps_deg_root = ps[5][0:1, 0:2 * N]
        ident = eye[:, 0, 0:P]

        edges_in, dw_in, bias0_in, bias1_in, bias2_in = (
            sem(n) for n in ("edges_in", "dw_in", "bias0_in", "bias1_in", "bias2_in"))
        x_in = [sem(f"x_in{t}") for t in range(NT)]
        unit_in = [sem(f"unit_in{u}") for u in range(UNITS)]
        stored = sem("stored")
        r_w0_done, b_base_done = sem("r_w0_done"), sem("b_base_done")
        iota_done, consts_done, rstd_done, dinv_done, rstd2_done, bias0_lo_done, bias2_lo_done = (
            sem(n) for n in ("iota_done", "consts_done", "rstd_done", "dinv_done", "rstd2_done", "bias0_lo_done",
                             "bias2_lo_done"))
        deg_root_done, root_hi_done, root_lo_done, floor_scale_done = (
            sem(n) for n in ("deg_root_done", "root_hi_done", "root_lo_done", "floor_scale_done"))
        hi_done = [sem(f"hi_done{u}") for u in range(UNITS)]
        lo_done = [sem(f"lo_done{u}") for u in range(UNITS)]
        table_ready, s_w1_done = sem("table_ready"), sem("s_w1_done")
        count_done = [sem(f"count_done{t}") for t in range(NT)]
        poly_hi_done = [sem(f"poly_hi_done{t}") for t in range(NT)]
        h0_done, bias0_hi_done, bias1_done, h0t_hi_done = (
            sem(n) for n in ("h0_done", "bias0_hi_done", "bias1_done", "h0t_hi_done"))
        b_hi_done, q_hi_done, relu_done, dinv_row_done, deg_root_parts_done, bias2_hi_done = (
            sem(n) for n in ("b_hi_done", "q_hi_done", "relu_done", "dinv_row_done", "deg_root_parts_done",
                             "bias2_hi_done"))
        h1_hi_done, agg_hi_done, z_done, v_hi_done, square_done, root_done = (
            sem(n) for n in ("h1_hi_done", "agg_hi_done", "z_done", "v_hi_done", "square_done",
                             "root_done"))
        ones_done, ident_done, m_t_done, r_hi_done, h1_norm_done = (
            sem(n) for n in ("ones_done", "ident_done", "m_t_done", "r_hi_done", "h1_norm_done"))
        eye_done, var_done, shift_done, onehot_done, h0t_lo_done, s_done, r_done = (
            sem(n) for n in ("eye_done", "var_done", "shift_done", "onehot_done", "h0t_lo_done", "s_done", "r_done"))
        b_sum_done, poly_lo_done, b_lo_done, q_lo_done, deg_done, dinv_eye_done = (
            sem(n) for n in ("b_sum_done", "poly_lo_done", "b_lo_done", "q_lo_done", "deg_done", "dinv_eye_done"))
        var2_done, shift2_done, h1_lo_done, agg_done = (
            sem(n) for n in ("var2_done", "shift2_done", "h1_lo_done", "agg_done"))
        z_hi_done, z_lo_done, v_lo_done, sum_done, scaled_done, dve_own = (
            sem(n) for n in ("z_hi_done", "z_lo_done", "v_lo_done", "sum_done", "scaled_done",
                             "dve_own"))
        x1_done = [sem(f"x1_done{t}") for t in range(NT)]
        half_done = [sem(f"half_done{k}") for k in range(2)]
        agg_hi0_done, agg_lo_done = sem("agg_hi0_done"), sem("agg_lo_done")
        counted, h0t_ps_done, bias1_ps_done, tr_ps_done, srs_ps_done, b_ps_done, q_ps_done = (
            sem(n) for n in ("counted", "h0t_ps_done", "bias1_ps_done", "tr_ps_done", "srs_ps_done", "b_ps_done",
                             "q_ps_done"))
        deg_ps_done, dinv_ps_done, deg_root_ps_done, bq_ps_done, agg_ps_done = (
            sem(n) for n in ("deg_ps_done", "dinv_ps_done", "deg_root_ps_done", "bq_ps_done", "agg_ps_done"))
        z_ps_done, z_used, v_ps_done, out_ps_done = (
            sem(n) for n in ("z_ps_done", "z_used", "v_ps_done", "out_ps_done"))

        w_rows = w.rearrange("(c p) n -> p c n", p=P)
        w1_rows = w1.rearrange("(c p) (u n) -> u p c n", p=P, n=D)
        w2_rows = w2.rearrange("(u c p) n -> u p c n", p=P, c=DT)
        x_rows = x.rearrange("(t p) d -> t p d", p=P)
        out_rows = out.rearrange("(t p) d -> t p d", p=P)

        def unit_dram(u):
            return w_rows if u == 0 else w1_rows[u - 1] if u <= UPM else w2_rows[u - 1 - UPM]

        def w_part(part, c):
            return part[:, slot[0], c, :]

        def w1_part(part, c, j):
            return part[:, slot[1 + j // PER], c, (j % PER) * P:(j % PER + 1) * P]

        def w2_part(part, j):
            return part[:, slot[1 + UPM + j // PER], j % PER, :]

        def work_feat(c):
            return work[:].rearrange("p t d -> p (t d)")[:, c * N:(c + 1) * N]

        def split_waits(eng, u):
            if u == UNITS - 2:
                eng.wait_ge(q_ps_done, NT)
            if u == UNITS - 1:
                eng.wait_ge(z_ps_done, PER)

        block = ctx.enter_context(nc.Block())

        @block.sync
        def _(sp):
            sp.dma_start(edge_i[:, 0, :], src.rearrange("(p t) -> p t", t=ET)).then_inc(edges_in, 16)
            for t in range(NT):
                sp.dma_start(x_sb[:, t, :], x_rows[t]).then_inc(x_in[t], 16)
            for u in range(UNITS):
                if u >= RAW:
                    sp.wait_ge(hi_done[u - RAW], DT)
                    sp.wait_ge(lo_done[u - RAW], DT)
                sp.dma_start(raw[:, u % RAW], unit_dram(u)).then_inc(unit_in[u], 16)
                if u == RAW - 1:
                    sp.dma_start(bias1_rows[:], b1.rearrange("(j p) -> j p", p=P)).then_inc(bias1_in, 16)
                    sp.dma_start(bias2[:], b2.rearrange("(o k) -> o k", o=1)).then_inc(bias2_in, 16)
            for t in range(NT):
                for k, at in enumerate(halves):
                    sp.wait_ge(half_done[k], t + 1)
                    sp.dma_start(out_rows[t][:, at], work[:, t, at]).then_inc(stored, 16)
            sp.wait_ge(stored, 16 * NT * len(halves))

        @block.gpsimd
        def _(pool):
            nc.gpsimd.iota(column[:], [[1, N], [0, 2]], base=0, channel_multiplier=0,
                           allow_small_or_imprecise_dtypes=True).then_inc(iota_done, 1)
            nc.gpsimd.iota(row[:], [[P, NT]], base=0, channel_multiplier=1,
                           allow_small_or_imprecise_dtypes=True).then_inc(iota_done, 1)
            nc.gpsimd.memset(minus_half[:], -0.5).then_inc(consts_done, 1)
            nc.gpsimd.memset(tiny[:], TINY).then_inc(consts_done, 1)
            pool.wait_ge(bias0_hi_done, 1)
            nc.gpsimd.tensor_tensor(bias0_lo, bias0, bias0_hi.bitcast(F32),
                                    ALU.subtract).then_inc(bias0_lo_done, 1)
            pool.wait_ge(consts_done, 1)
            pool.wait_ge(var_done, 1)
            nc.gpsimd.tensor_tensor(rstd[:], var_eps[:], minus_half[:], ALU.pow).then_inc(rstd_done, 1)

            def split_lo(u, c):
                pool.wait_ge(hi_done[u], c + 1)
                split_waits(pool, u)
                nc.gpsimd.tensor_tensor(wt_lo[:, slot[u], c, :], raw[:, u % RAW, c, :],
                                        wt_hi[:, slot[u], c, :].bitcast(F32), ALU.subtract).then_inc(lo_done[u], 1)

            for c in range(DT):
                split_lo(0, c)
            for c in range(DT - 1):
                split_lo(1, c)
            pool.wait_ge(dw_in, 16)
            pool.wait_ge(s_done, NT)
            nc.gpsimd.tensor_scalar(r_w0[:], row_sum[:], dw_sb[:, 0:1], 0.0, ALU.mult, ALU.add).then_inc(r_w0_done, 1)
            pool.wait_ge(r_w0_done, 1)
            for t in range(NT):
                nc.gpsimd.tensor_scalar(b_sum[:, t, :], eye[:, t, :], r_w0[:, t:t + 1], 0.0, ALU.mult,
                                        ALU.add).then_inc(b_base_done, 1)
            for t in range(NT):
                pool.wait_ge(b_base_done, t + 1)
                pool.wait_ge(s_w1_done, 1)
                nc.gpsimd.tensor_tensor(b_sum[:, t, :], b_sum[:, t, :], s_w1[:, t, :],
                                        ALU.add).then_inc(b_base_done, 1)
            split_lo(1, DT - 1)
            pool.wait_ge(deg_done, NT)
            nc.gpsimd.tensor_tensor(dinv[:], deg[:], minus_half[:], ALU.pow).then_inc(dinv_done, 1)
            pool.wait_ge(dinv_done, 1)
            nc.gpsimd.tensor_tensor(deg_root[:], deg[:], dinv[:], ALU.mult).then_inc(deg_root_done, 1)
            pool.wait_ge(deg_root_done, 1)
            nc.gpsimd.tensor_copy(root_hi[:], deg_root[:]).then_inc(root_hi_done, 1)
            pool.wait_ge(root_hi_done, 1)
            nc.gpsimd.tensor_tensor(root_lo[:], deg_root[:], root_hi[:].bitcast(F32),
                                    ALU.subtract).then_inc(root_lo_done, 1)
            nc.gpsimd.tensor_scalar(floor_scale[:], dinv[:], 1.0 / NORM_FLOOR, 0.0, ALU.mult,
                                    ALU.add).then_inc(floor_scale_done, 1)
            for c in range(DT - 1):
                split_lo(2, c)
            pool.wait_ge(relu_done, 2)
            nc.gpsimd.tensor_tensor(x_sb[:, 1, :], temp[:, 1, :], x_sb[:, 1, :], ALU.add).then_inc(x1_done[1], 1)
            for t in range(NT):
                at = slice(t, t + 1)
                pool.wait_ge(var2_done, t + 1)
                nc.gpsimd.tensor_tensor(rstd2[:, at], var_eps2[:, at], minus_half[:, at],
                                        ALU.pow).then_inc(rstd2_done, 1)
            for u in (3, 5, 4, *range(6, UNITS)):
                for c in range(DT):
                    split_lo(u, c)
            for t in range(NT):
                pool.wait_ge(scaled_done, t + 1)
                nc.gpsimd.tensor_tensor(work[:, t, halves[0]], temp[:, t, halves[0]], x_sb[:, t, halves[0]],
                                        ALU.add).then_inc(half_done[0], 1)

        @block.scalar
        def _(act):
            act.dma_start(edge_i[:, 1, :], dst.rearrange("(p t) -> p t", t=ET)).then_inc(edges_in, 16)
            act.dma_start(dw_sb[:], dw.partition_broadcast(P)).then_inc(dw_in, 16)
            act.dma_start(bias0, b.rearrange("(o k) -> o k", o=1)).then_inc(bias0_in, 16)

            def split_hi(u, c):
                if c == 0:
                    act.wait_ge(unit_in[u], 16)
                    split_waits(act, u)
                nc.scalar.activation(wt_hi[:, slot[u], c, :], raw[:, u % RAW, c, :], ACT.Copy).then_inc(hi_done[u], 1)

            act.wait_ge(ones_done, 1)
            nc.scalar.activation(ready[:], ones_r[:, 0:1].bitcast(F32), ACT.Sqrt).then_inc(table_ready, 1)
            act.wait_ge(bias0_in, 16)
            nc.scalar.activation(bias0_hi, bias0, ACT.Copy).then_inc(bias0_hi_done, 1)
            act.wait_ge(shift_done, 1)
            for t in range(NT):
                nc.scalar.activation(work[:, t, :], x_sb[:, t, :], ACT.Relu, bias=shift[:, t:t + 1],
                                     scale=rstd[:, t:t + 1]).then_inc(h0_done, 1)
            for c in range(2):
                split_hi(0, c)
            for t in range(2):
                act.wait_ge(h0t_ps_done, t + 1)
                nc.scalar.activation(feat_hi[:, 2 * t:2 * t + 2, :], ps_h0t[t][:].rearrange("p (c n) -> p c n", n=N),
                                     ACT.Copy).then_inc(h0t_hi_done, 1)
                split_hi(0, 2 + t)
            for c in range(DT):
                split_hi(1, c)
            for c in range(2):
                split_hi(2, c)
            act.wait_ge(counted, PAIRS)
            nc.scalar.activation(count_b[:, 0, :], ps_count[0][:, 0:N], ACT.Copy).then_inc(count_done[0], 1)

            def q_hi(t):
                act.wait_ge(q_ps_done, t + 1)
                nc.scalar.activation(node_hi[:, t, :], ps_q[t][:], ACT.Copy).then_inc(q_hi_done, 1)

            act.wait_ge(r_hi_done, 1)
            nc.scalar.activation(poly_hi[:, 0, :], s_adj[:, 0, :].bitcast(F32), ACT.Copy,
                                 scale=r_hi[:, 0:1].bitcast(F32)).then_inc(poly_hi_done[0], 1)
            act.wait_ge(dw_in, 16)
            nc.scalar.activation(s_w1, s_adj[:].bitcast(F32), ACT.Copy, scale=dw_sb[:, 1:2]).then_inc(s_w1_done, 1)
            q_hi(0)
            split_hi(2, 2)
            act.wait_ge(r_done, 1)
            for t in range(NT):
                act.wait_ge(srs_ps_done, t + 1)
                nc.scalar.activation(poly_hi[:, t, :], ps_srs[t][:, 0:N], ACT.Copy,
                                     scale=r_w3[:, t:t + 1]).then_inc(poly_hi_done[t], 1)
            for t in range(NT):
                act.wait_ge(deg_ps_done, t + 1)
                nc.scalar.activation(deg[:, t:t + 1], ps_deg[t][:, 0:1], ACT.Copy).then_inc(deg_done, 1)
            split_hi(2, 3)
            for t in range(NT):
                act.wait_ge(b_sum_done, t + 1)
                nc.scalar.activation(b_hi[:, t, :], b_sum[:, t, :], ACT.Copy).then_inc(b_hi_done, 1)
            q_hi(1)
            act.wait_ge(bias2_in, 16)
            nc.scalar.activation(bias2_hi, bias2[:], ACT.Copy).then_inc(bias2_hi_done, 1)
            for c in range(2):
                split_hi(3, c)
            for t in range(NT):
                act.wait_ge(bq_ps_done, t + 1)
                nc.scalar.activation(temp[:, t, :], ps_bq[t][:], ACT.Relu,
                                     scale=r_inv[:, t:t + 1]).then_inc(relu_done, 1)
            act.wait_ge(dinv_ps_done, 1)
            nc.scalar.activation(dinv_row[:], ps_dinv, ACT.Copy).then_inc(dinv_row_done, 1)
            split_hi(3, 2)
            act.wait_ge(deg_root_ps_done, 1)
            nc.scalar.activation(deg_root_parts, ps_deg_root, ACT.Copy).then_inc(deg_root_parts_done, 1)
            act.wait_ge(bias1_ps_done, 1)
            nc.scalar.activation(bias1[:], ps_bias1, ACT.Copy).then_inc(bias1_done, 1)
            split_hi(3, 3)
            for t in range(NT):
                act.wait_ge(shift2_done, t + 1)
                nc.scalar.activation(node_hi[:, t, :], x_sb[:, t, :], ACT.Relu, bias=shift2[:, t:t + 1],
                                     scale=scale2[:, t:t + 1]).then_inc(h1_hi_done, 1)
            for c in range(2):
                split_hi(4, c)
            for i, c in enumerate(AGG_ORDER[:-1]):
                act.wait_ge(agg_done, i + 1)
                nc.scalar.activation(feat_hi[:, c, :], work_feat(c), ACT.Copy).then_inc(agg_hi_done, 1)
            for c in range(2):
                split_hi(5, c)
            for j in range(HT):
                act.wait_ge(z_ps_done, j + 1)
                if j >= ZR:
                    act.wait_ge(z_lo_done, j - ZR + 1)
                if j == 0:
                    act.wait_ge(bias1_done, 1)
                nc.scalar.activation(z_sb[:, j % ZR, :], ps_z[j % ZR][:, 0:N], ACT.Relu,
                                     bias=bias1[:, j:j + 1]).then_inc(z_done, 1)
                if j == 0:
                    for c in range(2, DT):
                        split_hi(5, c)
                if j == 1:
                    for c in range(2, DT):
                        split_hi(4, c)
                u = 6 + (j - 3) // 2
                if j >= 3 and u < UNITS:
                    for c in range(DT // 2):
                        split_hi(u, (j - 3) % 2 * (DT // 2) + c)
            for i, (t, at, bank) in enumerate(V_PARTS):
                act.wait_ge(v_ps_done, i + 1)
                nc.scalar.activation(node_hi[:, t, at], bank[:, 0:at.stop - at.start], ACT.Copy,
                                     scale=dinv[:, t:t + 1]).then_inc(v_hi_done, 1)
            for k, at in enumerate(halves):
                act.wait_ge(out_ps_done, k + 1)
                nc.scalar.activation(temp[:, :, at], ps_out[k][:].rearrange("p (t k) -> p t k", t=NT),
                                     ACT.Square).then_inc(square_done, 1)
            for k in range(len(halves)):
                act.wait_ge(sum_done, k + 1)
                nc.scalar.activation(root[:, k], total[:, k], ACT.Sqrt, bias=tiny[:]).then_inc(root_done, 1)

        @block.vector
        def _(dve):
            own = [0]

            def mine(ins):
                own[0] += 1
                ins.then_inc(dve_own, 1)
                return own[0]

            def after(ins):
                dve.wait_ge(dve_own, mine(ins))

            nc.vector.memset(ones_r[:].bitcast(F32), 1.0).then_inc(ones_done, 1)
            dve.wait_ge(iota_done, 2)
            for t in range(NT):
                nc.vector.tensor_scalar(eye[:, t, :], column[:, :, 0], row[:, t:t + 1], None,
                                        ALU.is_equal).then_inc(eye_done, 1)
            dve.wait_ge(eye_done, NT)
            nc.vector.tensor_copy(ident_b[:], ident).then_inc(ident_done, 1)
            dve.wait_ge(edges_in, 32)
            after(nc.vector.tensor_copy(edge_b[:].rearrange("p q s e -> p s q e"),
                                        edge_i[:].rearrange("p s (q e) -> p s q e", e=2)))

            def onehot(g):
                q, n = sum(GROUPS[:g]), GROUPS[g]
                if q + n > ONEHOTS:
                    dve.wait_ge(counted, q + n - ONEHOTS)
                full = [P, 2 * n, N, 2]
                nc.vector.tensor_tensor(
                    onehots[:, q % ONEHOTS:q % ONEHOTS + n].rearrange("p q s v e -> p (q s) v e"),
                    edge_b[:, q:q + n].rearrange("p q s e -> p (q s) e").unsqueeze(2).broadcast_to(full),
                    column[:].unsqueeze(1).broadcast_to(full), ALU.is_equal).then_inc(onehot_done, n)

            onehot(0)
            for t in range(NT):
                dve.wait_ge(x_in[t], 16)
                n_stats = mine(nc.vector.bn_stats(stats[:, t, :], x_sb[:, t, :]))
            dve.wait_ge(dve_own, n_stats)
            for t in range(NT):
                n_aggr = mine(nc.vector.bn_aggr(mean_var[:, t, :], stats[:, t, :]))
            dve.wait_ge(dve_own, n_aggr)
            nc.vector.tensor_scalar(var_eps[:], mean_var[:, :, 1], EPS, None, ALU.add).then_inc(var_done, 1)
            onehot(1)
            dve.wait_ge(rstd_done, 1)
            nc.vector.scalar_tensor_tensor(out=shift[:], in0=mean_var[:, :, 0], scalar=-1.0, in1=rstd[:],
                                           op0=ALU.mult, op1=ALU.mult).then_inc(shift_done, 1)
            for g in range(2, len(GROUPS)):
                onehot(g)
            for k in range(2):
                dve.wait_ge(h0t_hi_done, k + 1)
                nc.vector.tensor_tensor(feat_lo[:, 2 * k:2 * k + 2, :],
                                        ps_h0t[k][:].rearrange("p (c n) -> p c n", n=N),
                                        feat_hi[:, 2 * k:2 * k + 2, :].bitcast(F32),
                                        ALU.subtract).then_inc(h0t_lo_done, 1)
            dve.wait_ge(counted, PAIRS)
            nc.vector.tensor_copy(count_b[:, 1, :], ps_count[1][:, 0:N]).then_inc(count_done[1], 1)
            for t in range(NT):
                dve.wait_ge(tr_ps_done, t + 1)
                nc.vector.scalar_tensor_tensor(out=s_adj[:, t, :], in0=ps_tr[t][:, 0:N], scalar=1.0,
                                               in1=eye[:, t, :], op0=ALU.min, op1=ALU.add,
                                               accum_out=row_sum[:, t:t + 1]).then_inc(s_done, 1)
            dve.wait_ge(s_done, NT)
            after(nc.vector.reciprocal(r_inv[:], row_sum[:]))
            nc.vector.tensor_copy(r_hi[:], r_inv[:]).then_inc(r_hi_done, 1)
            dve.wait_ge(dw_in, 16)
            nc.vector.tensor_scalar(r_w3[:], r_inv[:], dw_sb[:, 3:4], None, ALU.mult).then_inc(r_done, 1)
            dve.wait_ge(r_hi_done, 1)
            n_lo = mine(nc.vector.tensor_tensor(r_lo[:], r_inv[:], r_hi[:].bitcast(F32), ALU.subtract))
            nc.vector.tensor_scalar(poly_hi[:, 1, :], s_adj[:, 1, :].bitcast(F32), r_hi[:, 1:2].bitcast(F32), None,
                                    ALU.mult).then_inc(poly_hi_done[1], 1)
            dve.wait_ge(dve_own, n_lo)
            for t in range(NT):
                nc.vector.tensor_scalar(poly_lo[:, t, :], s_adj[:, t, :].bitcast(F32), r_lo[:, t:t + 1], None,
                                        ALU.mult).then_inc(poly_lo_done, 1)

            def q_lo(t):
                dve.wait_ge(q_hi_done, t + 1)
                nc.vector.tensor_tensor(node_lo[:, t, :], ps_q[t][:], node_hi[:, t, :].bitcast(F32),
                                        ALU.subtract).then_inc(q_lo_done, 1)

            for t in range(NT):
                dve.wait_ge(count_done[t], 1)
                nc.vector.tensor_tensor(m_t[:, t, :], ps_count[t][:, 0:N], eye[:, t, :],
                                        ALU.add).then_inc(m_t_done, 1)
            q_lo(0)
            for t in range(NT):
                dve.wait_ge(poly_hi_done[t], 2)
                nc.vector.scalar_tensor_tensor(out=poly_lo[:, t, :], in0=ps_srs[t][:, 0:N], scalar=r_w3[:, t:t + 1],
                                               in1=poly_hi[:, t, :].bitcast(F32), op0=ALU.mult,
                                               op1=ALU.subtract).then_inc(poly_lo_done, 1)
            for t in range(NT):
                dve.wait_ge(b_base_done, NT + t + 1)
                n_b = mine(nc.vector.scalar_tensor_tensor(out=b_sum[:, t, :], in0=ps_srs[t][:, 0:N],
                                                          scalar=dw_sb[:, 2:3],
                                                          in1=b_sum[:, t, :], op0=ALU.mult, op1=ALU.add))
            for t in range(NT):
                dve.wait_ge(dve_own, n_b - NT + 1 + t)
                dve.wait_ge(b_ps_done, t + 1)
                nc.vector.tensor_tensor(b_sum[:, t, :], ps_b[t][:, 0:N], b_sum[:, t, :],
                                        ALU.add).then_inc(b_sum_done, 1)
            for t in range(NT):
                dve.wait_ge(b_hi_done, t + 1)
                nc.vector.tensor_tensor(b_lo[:, t, :], b_sum[:, t, :], b_hi[:, t, :].bitcast(F32),
                                        ALU.subtract).then_inc(b_lo_done, 1)
            q_lo(1)
            for t in range(NT):
                dve.wait_ge(dinv_done, 1)
                nc.vector.tensor_scalar(dinv_eye[:, t, :], ident, dinv[:, t:t + 1], None,
                                        ALU.mult).then_inc(dinv_eye_done, 1)
            dve.wait_ge(hi_done[2], DT)
            nc.vector.tensor_tensor(wt_lo[:, slot[2], DT - 1, :], raw[:, 2 % RAW, DT - 1, :],
                                    wt_hi[:, slot[2], DT - 1, :].bitcast(F32), ALU.subtract).then_inc(lo_done[2], 1)
            dve.wait_ge(bias2_hi_done, 1)
            nc.vector.tensor_tensor(bias2_lo, bias2[:], bias2_hi.bitcast(F32),
                                    ALU.subtract).then_inc(bias2_lo_done, 1)

            def x1_stats(t):
                dve.wait_ge(x1_done[t], 1)
                return mine(nc.vector.bn_stats(stats2[:, t, :], x_sb[:, t, :]))

            def x1_moments(t, n_stats):
                dve.wait_ge(dve_own, n_stats)
                return mine(nc.vector.bn_aggr(mean_var2[:, t, :], stats2[:, t, :]))

            def x1_var(t, n_moments):
                dve.wait_ge(dve_own, n_moments)
                nc.vector.tensor_scalar(var_eps2[:, t:t + 1], mean_var2[:, t, 1:2], EPS, None,
                                        ALU.add).then_inc(var2_done, 1)

            def x1_scale(t):
                at = slice(t, t + 1)
                dve.wait_ge(rstd2_done, t + 1)
                return mine(nc.vector.tensor_tensor(scale2[:, at], rstd2[:, at], dinv[:, at], ALU.mult))

            def x1_shift(t, n_scale):
                at = slice(t, t + 1)
                dve.wait_ge(dve_own, n_scale)
                nc.vector.scalar_tensor_tensor(out=shift2[:, at], in0=mean_var2[:, t, 0:1], scalar=-1.0,
                                               in1=scale2[:, at],
                                               op0=ALU.mult, op1=ALU.mult).then_inc(shift2_done, 1)

            def x1_norm(t):
                nc.vector.tensor_scalar(temp[:, t, :], x_sb[:, t, :], mean_var2[:, t, 0:1], scale2[:, t:t + 1],
                                        ALU.subtract, ALU.mult).then_inc(h1_norm_done, 1)

            def h1_lo(t):
                dve.wait_ge(h1_norm_done, t + 1)
                dve.wait_ge(h1_hi_done, t + 1)
                for k in range(2):
                    at = slice(k * HALF, (k + 1) * HALF)
                    nc.vector.scalar_tensor_tensor(out=node_lo[:, t, at], in0=temp[:, t, at], scalar=0.0,
                                                   in1=node_hi[:, t, at].bitcast(F32), op0=ALU.max,
                                                   op1=ALU.subtract).then_inc(h1_lo_done, 1)

            dve.wait_ge(relu_done, 1)
            nc.vector.tensor_tensor(x_sb[:, 0, :], temp[:, 0, :], x_sb[:, 0, :], ALU.add).then_inc(x1_done[0], 1)
            n_stats0 = x1_stats(0)
            n_moments0 = x1_moments(0, n_stats0)
            x1_var(0, n_moments0)
            n_stats1 = x1_stats(1)
            n_scale0 = x1_scale(0)
            n_moments1 = x1_moments(1, n_stats1)
            x1_shift(0, n_scale0)
            x1_var(1, n_moments1)
            x1_norm(0)
            x1_shift(1, x1_scale(1))
            h1_lo(0)
            x1_norm(1)
            h1_lo(1)

            dve.wait_ge(dinv_row_done, 1)
            dve.wait_ge(agg_ps_done, 1)
            nc.vector.tensor_tensor(feat_hi[:, 0, :], ps_agg[0][:, 0:N], dinv_row[:], ALU.mult).then_inc(agg_hi0_done, 1)
            for c in AGG_ORDER:
                dve.wait_ge(agg_ps_done, c + 1)
                nc.vector.tensor_tensor(work_feat(c), ps_agg[c][:, 0:N], dinv_row[:], ALU.mult).then_inc(agg_done, 1)
            for i, c in enumerate(AGG_ORDER):
                if c == 0:
                    dve.wait_ge(agg_hi0_done, 1)
                    dve.wait_ge(agg_done, DT)
                else:
                    dve.wait_ge(agg_hi_done, i + 1)
                nc.vector.tensor_tensor(feat_lo[:, c, :], work_feat(c), feat_hi[:, c, :].bitcast(F32),
                                        ALU.subtract).then_inc(agg_lo_done, 1)
            for j in range(HT):
                dve.wait_ge(z_done, j + 1)
                if j >= ZR:
                    dve.wait_ge(z_used, j - ZR + 1)
                nc.vector.tensor_copy(z_hi[:, j % ZR, :], z_sb[:, j % ZR, :]).then_inc(z_hi_done, 1)
                dve.wait_ge(z_hi_done, j + 1)
                nc.vector.tensor_tensor(z_lo[:, j % ZR, :], z_sb[:, j % ZR, :], z_hi[:, j % ZR, :].bitcast(F32),
                                        ALU.subtract).then_inc(z_lo_done, 1)
            for i, (t, at, bank) in enumerate(V_PARTS):
                dve.wait_ge(v_hi_done, i + 1)
                nc.vector.scalar_tensor_tensor(out=node_lo[:, t, at], in0=bank[:, 0:at.stop - at.start],
                                               scalar=dinv[:, t:t + 1], in1=node_hi[:, t, at].bitcast(F32),
                                               op0=ALU.mult, op1=ALU.subtract).then_inc(v_lo_done, 1)
            for k, at in enumerate(halves):
                dve.wait_ge(square_done, k + 1)
                nc.vector.tensor_reduce(total[:, k], temp[:, :, at].rearrange("p t (g k) -> p t g k", k=GROUP),
                                        AX.X, ALU.add).then_inc(sum_done, 1)
            limit = floor_scale[:].unsqueeze(2).broadcast_to([P, NT, NG // 2])
            dve.wait_ge(floor_scale_done, 1)

            def inverse(k):
                dve.wait_ge(root_done, k + 1)
                return mine(nc.vector.reciprocal(inv[:, k], root[:, k]))

            def minus_half_total(k, n_before):
                dve.wait_ge(dve_own, n_before)
                dve.wait_ge(sum_done, k + 1)
                return mine(nc.vector.scalar_tensor_tensor(out=step_a[:, k], in0=total[:, k], scalar=-0.5,
                                                           in1=inv[:, k],
                                                           op0=ALU.mult, op1=ALU.mult))

            def times_inverse(k, n_before):
                dve.wait_ge(dve_own, n_before)
                return mine(nc.vector.tensor_tensor(step_b[:, k], step_a[:, k], inv[:, k], ALU.mult))

            def corrected(k, n_before):
                dve.wait_ge(dve_own, n_before)
                return mine(nc.vector.scalar_tensor_tensor(out=scale[:, k], in0=step_b[:, k], scalar=1.5,
                                                           in1=inv[:, k],
                                                           op0=ALU.add, op1=ALU.mult))

            def limited(k, n_before):
                dve.wait_ge(dve_own, n_before)
                return mine(nc.vector.tensor_tensor(factor[:, k], scale[:, k], limit, ALU.min))

            n0 = minus_half_total(0, inverse(0))
            n0 = times_inverse(0, n0)
            n1 = inverse(1)
            n0 = corrected(0, n0)
            n1 = minus_half_total(1, n1)
            n0 = limited(0, n0)
            n1 = times_inverse(1, n1)
            def scaled(k, t, n_before):
                dve.wait_ge(dve_own, n_before)
                nc.vector.tensor_tensor(
                    temp[:, t, halves[k]].rearrange("p (g k) -> p g k", k=GROUP),
                    factor[:, k, t].unsqueeze(2).broadcast_to([P, NG // 2, GROUP]),
                    ps_out[k][:, t * HALF:(t + 1) * HALF].rearrange("p (g k) -> p g k", k=GROUP),
                    ALU.mult).then_inc(scaled_done, 1)

            scaled(0, 0, n0)
            n1 = corrected(1, n1)
            scaled(0, 1, n0)
            n1 = limited(1, n1)
            for t in range(NT):
                scaled(1, t, n1)
            for t in range(NT):
                dve.wait_ge(scaled_done, NT + t + 1)
                nc.vector.tensor_tensor(work[:, t, halves[1]], temp[:, t, halves[1]], x_sb[:, t, halves[1]],
                                        ALU.add).then_inc(half_done[1], 1)

        @block.tensor
        def _(pe):
            def product(bank, terms, done=None, start=True, stop=True, skip_group_check=False):
                for i, (stationary, moving) in enumerate(terms):
                    last = nc.tensor.matmul(bank, stationary, moving, start=start and i == 0,
                                            stop=stop and i == len(terms) - 1, skip_group_check=skip_group_check)
                if done is not None:
                    last.then_inc(done, 1)

            def q_terms(t):
                at = slice(t * P, (t + 1) * P)
                return ([(ones_r[0:1, :], bias0_hi), (ones_r[0:1, :], bias0_lo)]
                        + [(feat_hi[:, c, at], w_part(wt_hi, c)) for c in range(DT)]
                        + [(feat_hi[:, c, at], w_part(wt_lo, c)) for c in range(DT)]
                        + [(feat_lo[:, c, at], w_part(wt_hi, c)) for c in range(DT)])

            terms = [q_terms(t) for t in range(NT)]
            LAST = len(terms[0])

            def q_part(t, first, end):
                product(ps_q[t][:], terms[t][first:end], q_ps_done if end == LAST else None, start=first == 0,
                        stop=end == LAST)

            def keep_warm(bank, count):
                for _ in range(count):
                    nc.tensor.matmul(bank[:, 0:N], filler[:, 0:P], filler, start=True, stop=True)

            pe.wait_ge(ones_done, 1)
            keep_warm(ps_q[0], WARM_START)
            pe.wait_ge(ident_done, 1)
            for q in range(PAIRS):
                pe.wait_ge(onehot_done, q + 1)
                for e in range(2):
                    for s in range(NT):
                        last = nc.tensor.matmul(ps_count[s][:, 0:N], onehots[:, q % ONEHOTS, 0, s * P:(s + 1) * P, e],
                                                onehots[:, q % ONEHOTS, 1, :, e], start=q + e == 0,
                                                stop=q == PAIRS - 1 and e == 1)
                last.then_inc(counted, 1)
                if q == 1:
                    pe.wait_ge(bias0_lo_done, 1)
                    for t in range(NT):
                        q_part(t, 0, 2)
                if q in (5, 7):
                    k = (q - 5) // 2
                    pe.wait_ge(h0_done, NT)
                    for c in (2 * k, 2 * k + 1):
                        for n in range(NT):
                            at = (c % 2) * N + n * P
                            last = nc.tensor.transpose(ps_h0t[k][:, at:at + P], work[:, n, c * P:(c + 1) * P], ident)
                    last.then_inc(h0t_ps_done, 1)
                if q in (11, 13):
                    k = (q - 11) // 2
                    pe.wait_ge(h0t_hi_done, k + 1)
                    pe.wait_ge(hi_done[0], 2 * k + 2)
                    q_part(0, 2 + 2 * k, 4 + 2 * k)
            q_part(1, 2, 4)
            for t in range(NT):
                pe.wait_ge(count_done[t], 1)
                nc.tensor.matmul(ps_tr[t][:, 0:N], ident_b[:], count_b[:, t, :], start=True, stop=False,
                                 skip_group_check=True)
                for s in range(NT):
                    pe.wait_ge(count_done[s], 1)
                    last = nc.tensor.matmul(ps_tr[t][:, s * P:(s + 1) * P], count_b[:, s, t * P:(t + 1) * P],
                                            ident_b[:],
                                            start=False, stop=s == NT - 1, skip_group_check=True)
                last.then_inc(tr_ps_done, 1)
            pe.wait_ge(lo_done[0], DT)
            q_part(0, 6, 10)
            pe.wait_ge(h0t_lo_done, 2)
            q_part(0, 10, LAST)

            def times_poly(banks, before, done):
                for c in range(NT):
                    pe.wait_ge(poly_hi_done[c], before + 1)
                    pe.wait_ge(poly_lo_done, before * NT + c + 1)
                    for m in range(NT):
                        at = slice(m * P, (m + 1) * P)
                        for part in (poly_hi, poly_lo):
                            last = nc.tensor.matmul(banks[m][:, 0:N], s_adj[:, c, at], part[:, c, :],
                                                    start=c == 0 and part is poly_hi,
                                                    stop=c == NT - 1 and part is poly_lo)
                        if c == NT - 1:
                            last.then_inc(done, 1)

            q_part(1, 4, 5)
            pe.wait_ge(s_done, NT)
            times_poly(ps_srs, 0, srs_ps_done)
            q_part(1, 5, 10)
            pe.wait_ge(m_t_done, NT)
            for t in range(NT):
                product(ps_deg[t], [(m_t[:, s, t * P:(t + 1) * P], ones_r[:, 0:2]) for s in range(NT)], deg_ps_done)
            times_poly(ps_b, 1, b_ps_done)
            q_part(1, 10, LAST)
            pe.wait_ge(deg_done, NT)
            for s in range(NT):
                for l, r, l_done, r_done in ((b_hi, node_hi, b_hi_done, q_hi_done),
                                             (b_lo, node_hi, b_lo_done, q_hi_done),
                                             (b_hi, node_lo, b_hi_done, q_lo_done)):
                    pe.wait_ge(l_done, s + 1)
                    pe.wait_ge(r_done, s + 1)
                    for t in range(NT):
                        final = s == NT - 1 and r is node_lo
                        product(ps_bq[t][:], [(l[:, s, t * P:(t + 1) * P], r[:, s, :])],
                                bq_ps_done if final else None, start=s == 0 and l is b_hi and r is node_hi,
                                stop=final)
            pe.wait_ge(dinv_eye_done, NT)
            for t in range(NT):
                last = nc.tensor.matmul(ps_dinv[:, t * P:(t + 1) * P], ones_r[:].bitcast(F32), dinv_eye[:, t, :],
                                        start=True, stop=True)
            last.then_inc(dinv_ps_done, 1)
            for k, (part, part_done) in enumerate(((root_hi[:].bitcast(F32), root_hi_done), (root_lo, root_lo_done))):
                pe.wait_ge(part_done, 1)
                for t in range(NT):
                    last = nc.tensor.matmul(ps_deg_root[:, k * N + t * P:k * N + (t + 1) * P], part[:, t:t + 1],
                                            ident,
                                            start=True, stop=True)
            last.then_inc(deg_root_ps_done, 1)
            pe.wait_ge(bias1_in, 16)
            nc.tensor.transpose(ps_bias1, bias1_rows[:], ident[0:HT, 0:HT]).then_inc(bias1_ps_done, 1)
            keep_warm(ps_z[1], WARM_NORM[0])
            pe.wait_ge(deg_root_parts_done, 1)
            pe.wait_ge(bias2_lo_done, 1)
            for k, cols in enumerate(halves):
                for t in range(NT):
                    root_hi_row, root_lo_row = (
                        deg_root_parts[:, half * N + t * P:half * N + (t + 1) * P] for half in range(2))
                    product(ps_out[k][:, t * HALF:(t + 1) * HALF],
                            [(root_hi_row, bias2_hi[:, cols]), (root_lo_row, bias2_hi[:, cols]),
                             (root_hi_row, bias2_lo[:, cols])], start=t == 0, stop=False,
                            skip_group_check=True)
            keep_warm(ps_z[1], WARM_NORM[1])
            pe.wait_ge(dinv_row_done, 1)
            for s in range(NT):
                pe.wait_ge(h1_hi_done, s + 1)
                for c in range(DT):
                    product(ps_agg[c][:, 0:N], [(node_hi[:, s, c * P:(c + 1) * P], m_t[:, s, :])],
                            start=s == 0, stop=False)
                for c in range(DT):
                    pe.wait_ge(h1_lo_done, 2 * s + c * P // HALF + 1)
                    product(ps_agg[c][:, 0:N], [(node_lo[:, s, c * P:(c + 1) * P], m_t[:, s, :])],
                            agg_ps_done if s == NT - 1 else None, start=False, stop=s == NT - 1)

            def hidden_high(j, c):
                product(ps_z[j % ZR][:, 0:N], [(w1_part(part, c, j), feat_hi[:, c, :]) for part in (wt_hi, wt_lo)],
                        start=c == 0, stop=False)

            def hidden_low(j, c, final):
                product(ps_z[j % ZR][:, 0:N], [(w1_part(wt_hi, c, j), feat_lo[:, c, :])],
                        z_ps_done if final else None, start=False, stop=final)

            def hidden(j):
                pe.wait_ge(lo_done[1 + j // PER], DT)
                pe.wait_ge(z_done, j - ZR + 1)
                for c in range(DT):
                    hidden_high(j, c)
                for c in range(DT):
                    hidden_low(j, c, c == DT - 1)

            def project(j, part, done=None):
                t, cols, bank = part
                pe.wait_ge(z_lo_done, j + 1)
                pe.wait_ge(lo_done[1 + UPM + j // PER], j % PER + 1)
                at = slice(t * P, (t + 1) * P)
                product(bank[:, 0:cols.stop - cols.start], [(l[:, j % ZR, at], w2_part(r, j)[:, cols])
                                     for l, r in ((z_hi, wt_hi), (z_lo, wt_hi), (z_hi, wt_lo))],
                        done, start=j == 0, stop=j == HT - 1)

            pe.wait_ge(lo_done[1], DT)
            for c, j in ((0, 0), (0, 1), (0, 2), (1, 0), (1, 1), (1, 2), (2, 0), (2, 1), (3, 0), (-1, 0), (3, 1),
                         (-1, 1), (2, 2), (3, 2), (-1, 2)):
                if c == 0:
                    pe.wait_ge(agg_hi0_done, 1)
                if c > 0:
                    pe.wait_ge(agg_hi_done, c)
                if (c, j) == (0, 2):
                    pe.wait_ge(agg_done, 1)
                if c >= 0:
                    hidden_high(j, c)
                else:
                    for i, low in enumerate(AGG_ORDER):
                        pe.wait_ge(agg_lo_done, i + 1)
                        hidden_low(j, low, low == AGG_ORDER[-1])
            LAG = 2
            for j in range(LAG, HT):
                if j >= ZR:
                    hidden(j)
                for part in V_PARTS:
                    project(j - LAG, part, z_used if part is V_PARTS[-1] else None)
            for part in V_PARTS:
                for j in range(HT - LAG, HT):
                    project(j, part, v_ps_done if j == HT - 1 else None)

            for k, s, low in ((0, 0, 0), (0, 1, 0), (1, 0, 0), (0, 0, 1), (0, 1, 1), (1, 1, 0), (1, 0, 1), (1, 1, 1)):
                pe.wait_ge((v_hi_done, v_lo_done)[low], 1 if s == 0 else 2 + k)
                final = (s, low) == (1, 1)
                for t in range(NT):
                    last = nc.tensor.matmul(ps_out[k][:, t * HALF:(t + 1) * HALF], m_t[:, s, t * P:(t + 1) * P],
                                            (node_hi, node_lo)[low][:, s, halves[k]], start=False,
                                            stop=final, skip_group_check=True)
                if final:
                    last.then_inc(out_ps_done, 1)


_INS = ['x', 'src', 'dst', 'L0_gnn_W', 'L0_gnn_b', 'L0_gnn_diffusion_weights', 'L1_gnn_W1', 'L1_gnn_b1', 'L1_gnn_W2',
        'L1_gnn_b2']


def kernel(**inputs):
    import numpy as _np
    import concourse.bacc as _bacc
    from concourse import mybir as _mybir
    from concourse.bass_utils import run_bass_kernel_spmd as _run

    nc = _bacc.Bacc("TRN2", target_bir_lowering=False, num_devices=1)
    arrays, args = {}, []
    for name in _INS:
        a = _np.ascontiguousarray(inputs[name])
        arrays[f"in_{name}"] = a
        args.append(nc.dram_tensor(f"in_{name}", a.shape, _mybir.dt.from_np(a.dtype), kind="ExternalInput").ap())
    out = nc.dram_tensor("out", inputs['x'].shape, _mybir.dt.float32, kind="ExternalOutput").ap()
    gnn_block(nc, *args, out)
    r = _run(nc, [arrays], core_ids=[0])
    return r.results[0]["out"]
```
